# Optimizing a Trainium2 kernel written in Bass

```python
import numpy as np
import jax
import jax.numpy as jnp

def _softmax(x, axis=-1):
    return jax.nn.softmax(x, axis=axis)

def _gelu(x):
    return jax.nn.gelu(x, approximate=True)

def _silu(x):
    return jax.nn.silu(x)

def _sigmoid(x):
    return jax.nn.sigmoid(x)

def _layernorm(x, axis=-1, eps=1e-05):
    m = jnp.mean(x, axis=axis, keepdims=True)
    v = jnp.var(x, axis=axis, keepdims=True)
    return (x - m) / jnp.sqrt(v + eps)

def _scatter_add(tgt, idx, src, axis=0):
    return tgt.at[idx].add(src)

def _segment_sum(src, seg, n):
    return jax.ops.segment_sum(src, seg, n)
kernel_name = 'mk_cond_resid_d2_seqx_r8_dc9c1e'

def setup_inputs(seed: int=0):
    np.random.seed(seed)
    _w = jnp.asarray

    def _rec_inputs():
        import jax
        import jax.numpy as jnp
        _rk = jax.random.key(seed)
        x = 0.0001044 + 1 * jax.random.normal(jax.random.fold_in(_rk, 1), (32, 128, 128), jnp.float32)
        _lenS = 128 - jax.random.randint(jax.random.fold_in(_rk, 7), (32,), 0, max(1, 128 // 4) + 1, jnp.int32)
        _lenS2 = 128 - jax.random.randint(jax.random.fold_in(_rk, 8), (32,), 0, max(1, 128 // 4) + 1, jnp.int32)
        cond_1024 = 0.00141218 + 0.997886 * jax.random.normal(jax.random.fold_in(_rk, 11), (32, 128), jnp.float32)
        return (x, cond_1024)
    x, cond_1024 = _rec_inputs()

    def _L0_cond_setup():
        import jax, jax.numpy as jnp
        import numpy as np
        B, T, C = (64, 64, 128)
        key = jax.random.key(seed)
        ks = jax.random.split(key, 17)
        s_in = 1.0 / np.sqrt(C)

        def lin(kw, kb, fan_in):
            s = 1.0 / np.sqrt(fan_in)
            W = jax.random.uniform(kw, (C, fan_in), jnp.float32, -s, s)
            b = jax.random.uniform(kb, (C,), jnp.float32, -s, s)
            return (W, b)
        Wxz, bxz = lin(ks[0], ks[1], C)
        Whz, bhz = lin(ks[2], ks[3], C)
        Wxr, bxr = lin(ks[4], ks[5], C)
        Whr, bhr = lin(ks[6], ks[7], C)
        Wxh, bxh = lin(ks[8], ks[9], C)
        Whh, bhh = lin(ks[10], ks[11], C)
        Whq, bhq = lin(ks[12], ks[13], C)
        X = jax.random.normal(ks[14], (B, T, C), jnp.float32)
        h0 = jax.random.normal(ks[15], (B, C), jnp.float32)
        return {'X': X, 'h0': h0, 'Wxz': Wxz, 'bxz': bxz, 'Whz': Whz, 'bhz': bhz, 'Wxr': Wxr, 'bxr': bxr, 'Whr': Whr, 'bhr': bhr, 'Wxh': Wxh, 'bxh': bxh, 'Whh': Whh, 'bhh': bhh, 'Whq': Whq, 'bhq': bhq}
    _L0_cond_all = _L0_cond_setup()
    _L0_cond_in = {k: v for k, v in _L0_cond_all.items() if k in ('Wxz', 'bxz', 'Whz', 'bhz', 'Wxr', 'bxr', 'Whr', 'bhr', 'Wxh', 'bxh', 'Whh', 'bhh', 'Whq', 'bhq')}
    del _L0_cond_all

    def _L1_cond_setup():
        import jax, jax.numpy as jnp
        import numpy as np
        TOP_K = 2
        N_EXPERTS = 8
        N_SHARED = 1
        EPS = 1e-09
        key = jax.random.key(seed)
        ks = jax.random.split(key, 10)
        B, T, d = (2, 256, 128)
        h_s, h_r, E = (256, 64, N_EXPERTS)
        return {'x': jax.random.normal(ks[0], (B, T, d), jnp.float32), 't_emb': jax.random.normal(ks[1], (B, d), jnp.float32), 'router_w': jax.random.normal(ks[2], (E, d), jnp.float32) * 0.01, 'router_t_w': jax.random.normal(ks[3], (E, d), jnp.float32) * 0.01, 'router_bias': jnp.zeros((E,), jnp.float32), 'sw1': jax.random.normal(ks[4], (h_s, d), jnp.float32) * 0.02, 'sw3': jax.random.normal(ks[5], (h_s, d), jnp.float32) * 0.02, 'sw2': jax.random.normal(ks[6], (d, h_s), jnp.float32) * 0.02, 'rw1': jax.random.normal(ks[7], (E, h_r, d), jnp.float32) * 0.02, 'rw2': jax.random.normal(ks[8], (E, d, h_r), jnp.float32) * 0.02}
    _L1_cond_all = _L1_cond_setup()
    _L1_cond_in = {k: v for k, v in _L1_cond_all.items() if k in ('router_w', 'router_t_w', 'router_bias', 'sw1', 'sw3', 'sw2', 'rw1', 'rw2')}
    del _L1_cond_all
    return {'x': x, 'cond_1024': cond_1024, 'L0_cond_Wxz': _L0_cond_in['Wxz'], 'L0_cond_bxz': _L0_cond_in['bxz'], 'L0_cond_Whz': _L0_cond_in['Whz'], 'L0_cond_bhz': _L0_cond_in['bhz'], 'L0_cond_Wxr': _L0_cond_in['Wxr'], 'L0_cond_bxr': _L0_cond_in['bxr'], 'L0_cond_Whr': _L0_cond_in['Whr'], 'L0_cond_bhr': _L0_cond_in['bhr'], 'L0_cond_Wxh': _L0_cond_in['Wxh'], 'L0_cond_bxh': _L0_cond_in['bxh'], 'L0_cond_Whh': _L0_cond_in['Whh'], 'L0_cond_bhh': _L0_cond_in['bhh'], 'L0_cond_Whq': _L0_cond_in['Whq'], 'L0_cond_bhq': _L0_cond_in['bhq'], 'L1_cond_router_w': _L1_cond_in['router_w'], 'L1_cond_router_t_w': _L1_cond_in['router_t_w'], 'L1_cond_router_bias': _L1_cond_in['router_bias'], 'L1_cond_sw1': _L1_cond_in['sw1'], 'L1_cond_sw3': _L1_cond_in['sw3'], 'L1_cond_sw2': _L1_cond_in['sw2'], 'L1_cond_rw1': _L1_cond_in['rw1'], 'L1_cond_rw2': _L1_cond_in['rw2']}

def reference(x, cond_1024, L0_cond_Wxz, L0_cond_bxz, L0_cond_Whz, L0_cond_bhz, L0_cond_Wxr, L0_cond_bxr, L0_cond_Whr, L0_cond_bhr, L0_cond_Wxh, L0_cond_bxh, L0_cond_Whh, L0_cond_bhh, L0_cond_Whq, L0_cond_bhq, L1_cond_router_w, L1_cond_router_t_w, L1_cond_router_bias, L1_cond_sw1, L1_cond_sw3, L1_cond_sw2, L1_cond_rw1, L1_cond_rw2):
    import jax
    import jax.numpy as jnp

    def _L0_cond_ref(X, h0, Wxz, bxz, Whz, bhz, Wxr, bxr, Whr, bhr, Wxh, bxh, Whh, bhh, Whq, bhq):
        import jax, jax.numpy as jnp
        import numpy as np
        B, T, C = (64, 64, 128)
        Xz = jnp.einsum('btc,hc->tbh', X, Wxz) + bxz
        Xr = jnp.einsum('btc,hc->tbh', X, Wxr) + bxr
        Xh = jnp.einsum('btc,hc->tbh', X, Wxh) + bxh

        def step(H, xs):
            xz, xr, xh = xs
            Z = jax.nn.sigmoid(xz + H @ Whz.T + bhz)
            R = jax.nn.sigmoid(xr + H @ Whr.T + bhr)
            H_tilda = jnp.tanh(xh + R * H @ Whh.T + bhh)
            H_new = Z * H + (1.0 - Z) * H_tilda
            Y = H_new @ Whq.T + bhq
            return (H_new, Y)
        _, Ys = jax.lax.scan(step, h0, (Xz, Xr, Xh))
        return jnp.transpose(Ys, (1, 0, 2))

    def _L1_cond_ref(x, t_emb, router_w, router_t_w, router_bias, sw1, sw3, sw2, rw1, rw2):
        import jax, jax.numpy as jnp
        import numpy as np
        TOP_K = 2
        N_EXPERTS = 8
        N_SHARED = 1
        EPS = 1e-09
        B, T, C = x.shape
        N = B * T
        x_flat = x.reshape(N, C)
        shared_out = jnp.einsum('nh,dh->nd', jax.nn.silu(x_flat @ sw1.T) * (x_flat @ sw3.T), sw2)
        t_bias = t_emb @ router_t_w.T
        t_bias_flat = jnp.broadcast_to(t_bias[:, None, :], (B, T, N_EXPERTS)).reshape(N, N_EXPERTS)
        s = jax.nn.sigmoid((x_flat @ router_w.T + t_bias_flat).astype(jnp.float32))
        sel_scores = s + router_bias
        _, topk_idx = jax.lax.top_k(sel_scores, TOP_K)
        s_sel = jnp.take_along_axis(s, topk_idx, axis=1)
        denom = jnp.sum(s_sel, axis=1, keepdims=True)
        gates = jnp.where(denom > EPS, s_sel / (denom + EPS), 1.0 / TOP_K).astype(x.dtype)
        combine = jnp.sum(gates[:, :, None] * jax.nn.one_hot(topk_idx, N_EXPERTS, dtype=x.dtype), axis=1)
        H = jax.nn.gelu(jnp.einsum('nd,ehd->enh', x_flat, rw1), approximate=False)
        O = jnp.einsum('enh,edh->end', H, rw2)
        routed_out = jnp.einsum('end,ne->nd', O, combine)
        out = (shared_out + routed_out) / (N_SHARED + TOP_K)
        return out.reshape(B, T, C)
    x = x + _L0_cond_ref(x, cond_1024, L0_cond_Wxz, L0_cond_bxz, L0_cond_Whz, L0_cond_bhz, L0_cond_Wxr, L0_cond_bxr, L0_cond_Whr, L0_cond_bhr, L0_cond_Wxh, L0_cond_bxh, L0_cond_Whh, L0_cond_bhh, L0_cond_Whq, L0_cond_bhq)
    x = x + _L1_cond_ref(x, cond_1024, L1_cond_router_w, L1_cond_router_t_w, L1_cond_router_bias, L1_cond_sw1, L1_cond_sw3, L1_cond_sw2, L1_cond_rw1, L1_cond_rw2)
    return x

_drawn_inputs = setup_inputs


def setup_inputs(seed=0):
    import zlib

    import numpy as np

    out = dict(_drawn_inputs(seed))
    spreads = {'L1_cond_router_bias': (0.0, 0.8)}
    factors = {'L0_cond_bxz': 8.0,
     'L0_cond_Whz': 3.508,
     'L0_cond_bhz': 8.0,
     'L0_cond_Wxr': 8.0,
     'L0_cond_bxr': 64.0,
     'L0_cond_Whr': 29.114,
     'L0_cond_bhr': 64.0,
     'L1_cond_router_w': 8.0,
     'L1_cond_router_t_w': 8.0,
     'L1_cond_sw1': 8.0,
     'L1_cond_sw3': 8.0,
     'L1_cond_sw2': 8.0,
     'L1_cond_rw1': 8.0,
     'L1_cond_rw2': 8.0}
    for name, (base, spread) in spreads.items():
        noise = np.random.default_rng([zlib.crc32(name.encode()), seed]).standard_normal(out[name].shape)
        drawn = base * np.exp(spread * noise) if base else spread * noise
        out[name] = jnp.asarray(drawn.astype(out[name].dtype))
    for name, factor in factors.items():
        out[name] = (out[name] * factor).astype(out[name].dtype)
    return out
```

```python
from contextlib import ExitStack

import concourse.bass as bass
from concourse import mybir

F32 = mybir.dt.float32
BF16 = mybir.dt.bfloat16
U32 = mybir.dt.uint32
ALU = mybir.AluOpType
ACT = mybir.ActivationFunctionType
AX_X = mybir.AxisListType.X

P = 128
B, T, C, E = 32, 128, 128, 8
GS = 8
GT = GS * B
GROUPS = T // GS
TILES = GT // P
SHARED = 2
PAIRS = 4
EPS = 1e-9
EULER = 2.718281828459045

W_Q = 0
W_SW1 = W_Q + C
W_SW3 = W_SW1 + SHARED * P
W_RW1 = W_SW3 + SHARED * P
W_SW2 = W_RW1 + PAIRS * P
W_RW2 = W_SW2 + SHARED * C
W_ROUTER = W_RW2 + PAIRS * C
W_ROUTER_T = W_ROUTER + E
W_END = W_ROUTER_T + E
S_COND = 0
S_BHQ = S_COND + P
S_RBIAS = S_BHQ + 1
S_IOTA = S_RBIAS + TILES * E
S_END = S_IOTA + TILES * E
R_KEPT, Z_KEPT, H_RESET, R_UPD, Z_UPD, RW_END = (P * i for i in range(6))


def gru_moe_program(nc: bass.Bass, x_t, w_in, w_rec, b_in, b_rec, w_moe, small, selectors, identity, out_t):
    with ExitStack() as ctx:
        def sb(name, shape, dtype=F32):
            return ctx.enter_context(nc.sbuf_tensor(name, shape, dtype))

        def sem(name):
            return ctx.enter_context(nc.semaphore(name))

        def bank(name):
            return ctx.enter_context(nc.psum_tensor(name, [P, 512], F32))

        x_ring = sb("x_ring", [P, 2, GT])
        w_in_sb = sb("w_in_sb", [P, 3 * P])
        w_rec_sb = sb("w_rec_sb", [P, 3 * P])
        w_scaled = sb("w_scaled", [P, RW_END])
        w_rest = sb("w_rest", [P, RW_END])
        w_split = sb("w_split", [P, 3, RW_END], BF16)
        moe_w = sb("moe_w", [P, W_END])
        small_sb = sb("small_sb", [P, S_END])
        sel_sb = sb("sel_sb", [3 * E, PAIRS, P], BF16)
        ident = sb("ident", [P, P], BF16)
        bias_rows = sb("bias_rows", [P, 2, 3 * P])
        bias_sum = sb("bias_sum", [P, 3 * P])
        bias_rest = sb("bias_rest", [P, 3 * P])
        bias_part = sb("bias_part", [P, 3, 3 * P], BF16)
        bias_w = sb("bias_w", [P, 3 * P], BF16)
        ones = sb("ones", [P, GT], BF16)
        table_in = sb("table_in", [P, 1])
        table_out = sb("table_out", [P, 1])
        tanh_r = sb("tanh_r", [P, B])
        tanh_z = sb("tanh_z", [P, B])
        cand = sb("cand", [P, B])
        reset = sb("reset", [P, B])
        reset_rest = sb("reset_rest", [P, B])
        reset_low = sb("reset_low", [P, B], BF16)
        kept = sb("kept", [P, B])
        kept_rest = sb("kept_rest", [P, B])
        kept_low = sb("kept_low", [P, B], BF16)
        upd = sb("upd", [P, B])
        upd_rest = sb("upd_rest", [P, B])
        upd_low = sb("upd_low", [P, B], BF16)
        g_hist = sb("g_hist", [P, 2, GT])
        x1 = sb("x1", [P, 2, GT])
        silu_tanh = sb("silu_tanh", [P, SHARED, GT])
        silu_a = sb("silu_a", [P, SHARED, GT])
        hid_s = sb("hid_s", [P, 2, SHARED, GT])
        gelu = sb("gelu", [P, PAIRS, GT])
        hid_r = sb("hid_r", [P, PAIRS, GT])
        out_sb = sb("out_sb", [P, 2, GT])
        t_bias = sb("t_bias", [P, TILES, E])
        euler = sb("euler", [P, TILES, E])
        unit = sb("unit", [P, TILES, E])
        epsilon = sb("epsilon", [P, TILES])
        neg_logit = sb("neg_logit", [P, TILES, E])
        exp_neg = sb("exp_neg", [P, TILES, E])
        one_plus = sb("one_plus", [P, TILES, E])
        score = sb("score", [P, TILES, E])
        sel_score = sb("sel_score", [P, TILES, E])
        top8 = sb("top8", [P, TILES, 8])
        top8_at = sb("top8_at", [P, TILES, 8], U32)
        first = sb("first", [P, TILES, E])
        second = sb("second", [P, TILES, E])
        mask = sb("mask", [P, TILES, E])
        chosen = sb("chosen", [P, TILES, E])
        denom = sb("denom", [P, TILES])
        denom_eps = sb("denom_eps", [P, TILES])
        inverse = sb("inverse", [P, TILES])
        gate_scale = sb("gate_scale", [P, TILES])
        even_gate = sb("even_gate", [P, TILES])
        by_score = sb("by_score", [P, TILES, E])
        by_half = sb("by_half", [P, TILES, E])
        combine = sb("combine", [P, TILES, E])
        comb_rest = sb("comb_rest", [P, TILES, E])
        comb_parts = sb("comb_parts", [P, TILES, 3, E], BF16)
        comb_t = sb("comb_t", [3 * E, GT], BF16)

        bank_r, bank_z, bank_h = bank("bank_r"), bank("bank_z"), bank("bank_h")
        work = [bank("work0"), bank("work1"), bank("work2")]
        bank_o = bank("bank_o")
        bank_m = bank("bank_m")
        y_ps = bank_m[:, 0:GT]
        score_ps = bank_m[:, GT:GT + TILES * E]
        comb_ps = bank_m[0:3 * E, 384:384 + GT // 2].bitcast(BF16)

        gru_loaded, bias_loaded, moe_loaded = sem("gru_loaded"), sem("bias_loaded"), sem("moe_loaded")
        x_loaded, out_free = [sem("x_loaded0"), sem("x_loaded1")], [sem("out_free0"), sem("out_free1")]
        setup_step, setup_done, zeroed = sem("setup_step"), sem("setup_done"), sem("zeroed")
        g_init, tb_ps_done, table_ready, moe_scaled = sem("g_init"), sem("tb_ps_done"), sem("table_ready"), sem("moe_scaled")
        r_pre, z_pre, h_pre = sem("r_pre"), sem("z_pre"), sem("h_pre")
        r_ready, z_ready, cand_ready = sem("r_ready"), sem("z_ready"), sem("cand_ready")
        reset_ready, kept_ready, upd_ready = sem("reset_ready"), sem("kept_ready"), sem("upd_ready")
        g_done = sem("g_done")
        y_done, scores_done, comb_t_done = sem("y_done"), sem("scores_done"), sem("comb_t_done")
        silu_pre, gelu_pre, out_done = sem("silu_pre"), sem("gelu_pre"), sem("out_done")
        silu_tanh_done, gelu_done, comb_copied = sem("silu_tanh_done"), sem("gelu_done"), sem("comb_copied")
        x1_done, silu_a_done, hid_s_done, hid_r_done = sem("x1_done"), sem("silu_a_done"), sem("hid_s_done"), sem("hid_r_done")
        final_done = sem("final_done")
        neg_done, score_done, top_done, top_at_done = sem("neg_done"), sem("score_done"), sem("top_done"), sem("top_at_done")
        picked_done, denom_done, inverse_done, scale_done = sem("picked_done"), sem("denom_done"), sem("inverse_done"), sem("scale_done")
        exp_done, one_plus_done, sel_done = sem("exp_done"), sem("one_plus_done"), sem("sel_done")
        constants_set, mask_done, chosen_done, denom_eps_done = sem("constants_set"), sem("mask_done"), sem("chosen_done"), sem("denom_eps_done")
        gated_done, combine_done, comb_rest_done, parts_done = sem("gated_done"), sem("combine_done"), sem("comb_rest_done"), sem("parts_done")

        def top_half(t):
            return t.bitcast(BF16)[:, 1::2]

        def over_groups(eng, group):
            group(0, 0, 0)
            group(1, 1, 1)
            with eng.Fori(1, GROUPS // 2 - 1) as pair:
                group(pair * 2, 0, None)
                group(pair * 2 + 1, 1, None)
            for k in range(GROUPS - 2, GROUPS + 2):
                group(k, k % 2, k)

        def has_steps(at):
            return at is None or at < GROUPS

        def has_next(at):
            return at is None or at < GROUPS - 1

        def has_a(at):
            return at is None or 1 <= at <= GROUPS

        def has_b(at):
            return at is None or at >= 2

        block = ctx.enter_context(nc.Block())

        @block.sync
        def _(sp):
            for half in out_free:
                sp.sem_inc(half, 16)
            sp.dma_start(w_rec_sb[:, :], w_rec).then_inc(gru_loaded, 16)
            sp.dma_start(w_in_sb[:, :], w_in).then_inc(gru_loaded, 16)
            for g in range(2):
                sp.dma_start(x_ring[:, g, :], x_t[:, g * GT:(g + 1) * GT]).then_inc(x_loaded[g], 16)
            sp.dma_start(moe_w[:, :], w_moe).then_inc(moe_loaded, 16)
            sp.dma_start(sel_sb[:, :, :], selectors).then_inc(moe_loaded, 16)
            sp.dma_start(ident[:, :], identity).then_inc(moe_loaded, 16)

            def group(k, parity, at):
                if has_a(at) and has_next(at):
                    sp.wait_ge(x1_done, k)
                    sp.dma_start(x_ring[:, 1 - parity, :],
                                 x_t[:, bass.ds((k + 1) * GT, GT)]).then_inc(x_loaded[1 - parity], 16)
                if has_b(at):
                    sp.wait_ge(final_done, k - 1)
                    sp.dma_start(out_t[:, bass.ds((k - 2) * GT, GT)],
                                 out_sb[:, parity, :]).then_inc(out_free[parity], 16)

            over_groups(sp, group)
            for half in out_free:
                sp.wait_ge(half, 16 + 16 * GROUPS // 2)

        @block.tensor
        def _(pe):
            def recur(dst, col, weights, data, part):
                for m in range(3 - part):
                    last = pe.matmul(dst[:, col:col + B], w_split[:, m, weights:weights + P], data,
                                     start=False, stop=True, skip_group_check=True)
                return last

            def project(dst, gate, parity):
                pe.matmul(dst[:, 0:GT], w_in_sb[:, gate * P:(gate + 1) * P], x_ring[:, parity, :],
                          start=True, stop=True, skip_group_check=True)
                pe.matmul(dst[:, 0:GT], bias_w[:, gate * P:(gate + 1) * P], ones[:, :],
                          start=False, stop=True, skip_group_check=True)

            def weights(col, width=P):
                return moe_w[:, col:col + width]

            def read_out(k, a):
                pe.wait_ge(g_done, k * GS)
                if not (type(k) is int and k == 1):
                    pe.wait_ge(comb_copied, k - 1)
                pe.matmul(y_ps, weights(W_Q), g_hist[:, a, :], start=True, stop=True).then_inc(y_done, 1)

            def router(k, a, tile):
                if tile == 0:
                    pe.wait_ge(x1_done, k)
                mm = pe.matmul(score_ps[:, tile * E:(tile + 1) * E], x1[:, a, tile * P:(tile + 1) * P],
                               weights(W_ROUTER, E), start=True, stop=True)
                if tile == TILES - 1:
                    mm.then_inc(scores_done, 1)

            def shared_hidden(k, a, chunk, with_b):
                if with_b:
                    pe.wait_ge(hid_r_done, (k - 2) * PAIRS + chunk + 1)
                dst = work[chunk]
                pe.matmul(dst[:, 0:GT], weights(W_SW1 + chunk * P), x1[:, a, :], start=True, stop=True)
                pe.matmul(dst[:, GT:2 * GT], weights(W_SW3 + chunk * P), x1[:, a, :],
                          start=True, stop=True).then_inc(silu_pre, 1)

            def routed_hidden(k, b, pair, with_a):
                if pair == 0:
                    pe.wait_ge(comb_copied, k - 1)
                elif pair == 1:
                    pe.wait_ge(hid_s_done, (k - 1) * SHARED)
                elif pair == 3 and with_a:
                    pe.wait_ge(hid_s_done, (k - 1) * SHARED + 1)
                elif pair == 3:
                    pe.wait_ge(hid_r_done, (k - 2) * PAIRS + 1)
                dst = work[(0, 1, 2, 0)[pair]]
                pe.matmul(dst[:, GT:2 * GT], sel_sb[:, pair, :], comb_t[:, :], start=True, stop=True)
                pe.matmul(dst[:, 0:GT], weights(W_RW1 + pair * P), x1[:, b, :],
                          start=True, stop=True).then_inc(gelu_pre, 1)

            def out_shared(k, b, chunk, with_a):
                if chunk == 0 and not with_a:
                    pe.wait_ge(final_done, k - 2)
                pe.wait_ge(hid_s_done, (k - 1) * SHARED)
                pe.matmul(bank_o[:, 0:GT], weights(W_SW2 + chunk * C), hid_s[:, b, chunk, :],
                          start=(chunk == 0), stop=False)

            def out_routed(k, pair):
                pe.wait_ge(hid_r_done, (k - 2) * PAIRS + pair + 1)
                mm = pe.matmul(bank_o[:, 0:GT], weights(W_RW2 + pair * C), hid_r[:, pair, :],
                               start=False, stop=(pair == PAIRS - 1))
                if pair == PAIRS - 1:
                    mm.then_inc(out_done, 1)

            def turn_gates(k):
                pe.wait_ge(parts_done, k)
                for tile in range(TILES):
                    mm = pe.transpose(comb_ps[:, tile * P:(tile + 1) * P],
                                      comb_parts[:, tile, :, :].rearrange("p m e -> p (m e)"), ident[:, :])
                mm.then_inc(comb_t_done, 1)

            pe.wait_ge(gru_loaded, 48)
            pe.wait_ge(setup_done, 1)
            pe.wait_ge(x_loaded[0], 16)
            for gate, dst in enumerate((bank_r, bank_z, bank_h)):
                project(dst, gate, 0)
            pe.matmul(bank_r[:, 0:B], w_rec_sb[:, 0:P], small_sb[:, S_COND:S_COND + B],
                      start=False, stop=True, skip_group_check=True).then_inc(r_pre, 1)
            pe.matmul(bank_z[:, 0:B], w_rec_sb[:, P:2 * P], small_sb[:, S_COND:S_COND + B],
                      start=False, stop=True, skip_group_check=True).then_inc(z_pre, 1)

            def group(k, parity, at):
                a, b = 1 - parity, parity

                def fill(slot):
                    if has_a(at):
                        if slot == (0, 0):
                            read_out(k, a)
                        if slot == (1, 0):
                            router(k, a, 0)
                        if slot == (1, 1):
                            router(k, a, 1)
                        if slot in ((2, 1), (3, 1)):
                            shared_hidden(k, a, slot[0] - 2, has_b(at))
                    if has_b(at):
                        if slot == (0, 1):
                            routed_hidden(k, b, 0, has_a(at))
                        if slot == (1, 1):
                            routed_hidden(k, b, 1, has_a(at))
                        if slot == (2, 0):
                            out_shared(k, b, 0, has_a(at))
                        if slot == (3, 0):
                            out_shared(k, b, 1, has_a(at))
                        if slot == (4, 0):
                            routed_hidden(k, b, 2, has_a(at))
                        if slot == (4, 1):
                            out_routed(k, 0)
                            out_routed(k, 1)
                        if slot == (5, 0):
                            routed_hidden(k, b, 3, has_a(at))
                        if slot == (6, 0):
                            out_routed(k, 2)
                        if slot == (7, 0):
                            out_routed(k, 3)
                    if has_a(at) and slot == (7, 1):
                        turn_gates(k)

                for s in range(GS):
                    nxt = ((s + 1) % GS) * B
                    if has_steps(at):
                        for part, data in enumerate((top_half(reset[:, :]), top_half(reset_rest[:, :]), reset_low[:, :])):
                            pe.wait_ge(reset_ready, (k * GS + s) * 3 + part + 1)
                            mm = recur(bank_h, s * B, H_RESET, data, part)
                        mm.then_inc(h_pre, 1)
                    if at == 0 and s == GS // 2:
                        pe.wait_ge(moe_scaled, 1)
                        pe.matmul(score_ps[:, 0:E], small_sb[:, S_COND:S_COND + P], weights(W_ROUTER_T, E),
                                  start=True, stop=True).then_inc(tb_ps_done, 1)
                    fill((s, 0))
                    if has_steps(at) and (has_next(at) or s < GS - 1):
                        pe.wait_ge(kept_ready, (k * GS + s) * 3 + 3)
                        for dst, w in ((bank_r, R_KEPT), (bank_z, Z_KEPT)):
                            for part, data in enumerate((top_half(kept[:, :]), top_half(kept_rest[:, :]), kept_low[:, :])):
                                recur(dst, nxt, w, data, part)
                        parts = (top_half(upd[:, :]), top_half(upd_rest[:, :]), upd_low[:, :])
                        for part, data in enumerate(parts):
                            pe.wait_ge(upd_ready, (k * GS + s) * 3 + part + 1)
                            mm = recur(bank_r, nxt, R_UPD, data, part)
                        mm.then_inc(r_pre, 1)
                        for part, data in enumerate(parts):
                            mm = recur(bank_z, nxt, Z_UPD, data, part)
                        mm.then_inc(z_pre, 1)
                    if has_next(at) and s == GS - 2:
                        pe.wait_ge(x_loaded[1 - parity], x_count(k, parity))
                        pe.wait_ge(r_ready, k * GS + GS)
                        project(bank_r, 0, 1 - parity)
                        pe.wait_ge(z_ready, k * GS + GS)
                        project(bank_z, 1, 1 - parity)
                    if has_next(at) and s == GS - 1:
                        pe.wait_ge(cand_ready, k * GS + GS)
                        project(bank_h, 2, 1 - parity)
                    fill((s, 1))

            def x_count(k, parity):
                return (k + 1 - (1 - parity)) * 8 + 16

            over_groups(pe, group)

        @block.scalar
        def _(act):
            act.dma_start(small_sb[:, :], small).then_inc(gru_loaded, 16)
            act.wait_ge(zeroed, 1)
            for m in range(3):
                act.dma_start(bias_rows[32 * m:32 * m + 1, 0, :], b_in).then_inc(bias_loaded, 16)
                act.dma_start(bias_rows[32 * m:32 * m + 1, 1, :], b_rec).then_inc(bias_loaded, 16)
            act.activation(table_out[:, :], table_in[:, :], ACT.Gelu).then_inc(table_ready, 1)

            def group(k, parity, at):
                def fill(slot):
                    if has_a(at):
                        if slot in ((3, 1), (4, 1)):
                            chunk = slot[0] - 3
                            act.wait_ge(silu_pre, (k - 1) * SHARED + chunk + 1)
                            act.activation(silu_tanh[:, chunk, :], work[chunk][:, 0:GT], ACT.Tanh,
                                           scale=0.5).then_inc(silu_tanh_done, 1)
                    if has_b(at):
                        pair = {(1, 1): 0, (2, 1): 1, (4, 1): 2, (5, 1): 3}.get(slot)
                        if pair is not None:
                            act.wait_ge(gelu_pre, (k - 2) * PAIRS + pair + 1)
                            act.activation(gelu[:, pair, :], work[(0, 1, 2, 0)[pair]][:, 0:GT],
                                           ACT.Gelu).then_inc(gelu_done, 1)

                for s in range(GS):
                    col = s * B
                    if has_steps(at):
                        act.wait_ge(r_pre, k * GS + s + 1)
                        act.activation(tanh_r[:, :], bank_r[:, col:col + B], ACT.Tanh, scale=0.5).then_inc(r_ready, 1)
                        act.wait_ge(z_pre, k * GS + s + 1)
                        act.activation(tanh_z[:, :], bank_z[:, col:col + B], ACT.Tanh, scale=0.5).then_inc(z_ready, 1)
                    if s == 0 and has_b(at):
                        act.wait_ge(comb_t_done, k - 1)
                        act.activation(comb_t[:, :], comb_ps, ACT.Copy).then_inc(comb_copied, 1)
                    if has_steps(at):
                        act.wait_ge(h_pre, k * GS + s + 1)
                        act.activation(cand[:, :], bank_h[:, col:col + B], ACT.Tanh).then_inc(cand_ready, 1)
                    fill((s, 1))

            over_groups(act, group)

        @block.vector
        def _(dve):
            done = [0]

            def then(ins):
                done[0] += 1
                ins.then_inc(setup_step, 1)
                dve.wait_ge(setup_step, done[0])

            dve.memset(table_in[:, :], 0.0)
            dve.memset(bias_rows[:, :, :], 0.0).then_inc(zeroed, 1)
            dve.memset(bias_w[:, :], 0.0)
            dve.memset(ones[:, :], 1.0)
            dve.wait_ge(gru_loaded, 48)
            dve.tensor_scalar(w_scaled[:, 0:3 * P], w_rec_sb[:, :], 0.25, None, ALU.mult)
            dve.tensor_scalar(g_hist[:, 1, GT - B:GT], small_sb[:, S_COND:S_COND + B], 2.0, None, ALU.mult).then_inc(g_init, 1)
            then(dve.tensor_scalar(w_scaled[:, 3 * P:5 * P], w_rec_sb[:, 0:2 * P], -0.5, None, ALU.mult))
            then(dve.tensor_copy(w_split[:, 0, :], w_scaled[:, :]))
            then(dve.tensor_tensor(w_rest[:, :], w_scaled[:, :], w_split[:, 0, :], ALU.subtract))
            then(dve.tensor_copy(w_split[:, 1, :], w_rest[:, :]))
            then(dve.tensor_tensor(w_split[:, 2, :], w_rest[:, :], w_split[:, 1, :], ALU.subtract))
            dve.wait_ge(bias_loaded, 96)
            then(dve.tensor_tensor(bias_sum[:, :], bias_rows[:, 0, :], bias_rows[:, 1, :], ALU.add))
            then(dve.tensor_copy(bias_part[:, 0, :], bias_sum[:, :]))
            then(dve.tensor_tensor(bias_rest[:, :], bias_sum[:, :], bias_part[:, 0, :], ALU.subtract))
            then(dve.tensor_copy(bias_part[:, 1, :], bias_rest[:, :]))
            then(dve.tensor_tensor(bias_part[:, 2, :], bias_rest[:, :], bias_part[:, 1, :], ALU.subtract))
            for m in range(3):
                ins = dve.tensor_copy(bias_w[32 * m:32 * m + 1, :], bias_part[32 * m:32 * m + 1, m, :])
            ins.then_inc(setup_done, 1)

            def experts_setup():
                dve.wait_ge(moe_loaded, 48)
                then(dve.tensor_scalar(moe_w[:, W_Q:W_Q + C], moe_w[:, W_Q:W_Q + C], 0.5, None, ALU.mult))
                dve.tensor_scalar(moe_w[:, W_SW2:W_RW2], moe_w[:, W_SW2:W_RW2], 0.5, None, ALU.mult).then_inc(moe_scaled, 1)

            def keep_cond_scores():
                dve.wait_ge(tb_ps_done, 1)
                for tile in range(TILES):
                    ins = dve.tensor_copy(t_bias[:, tile, :], score_ps[:, 0:E])
                then(ins)

            def group(k, parity, at):
                a, b = 1 - parity, parity

                def fill(slot):
                    if has_b(at):
                        pair = {(1, 1): 0, (2, 1): 1, (5, 1): 2, (6, 1): 3}.get(slot)
                        if pair is not None:
                            dve.wait_ge(gelu_done, (k - 2) * PAIRS + pair + 1)
                            dve.tensor_tensor(hid_r[:, pair, :], gelu[:, pair, :],
                                              work[(0, 1, 2, 0)[pair]][:, GT:2 * GT], ALU.mult).then_inc(hid_r_done, 1)
                    if has_a(at):
                        if slot == (0, 1):
                            if not has_steps(at):
                                dve.wait_ge(final_done, k - 2)
                            dve.wait_ge(y_done, k)
                            dve.scalar_tensor_tensor(out=x1[:, a, :], in0=y_ps, scalar=small_sb[:, S_BHQ:S_BHQ + 1],
                                                     in1=x_ring[:, a, :], op0=ALU.add, op1=ALU.add).then_inc(x1_done, 1)
                        if slot == (2, 0):
                            dve.wait_ge(scores_done, k)
                            dve.scalar_tensor_tensor(out=neg_logit[:, :, :],
                                                     in0=score_ps.rearrange("p (t e) -> p t e", e=E), scalar=-1.0,
                                                     in1=t_bias[:, :, :], op0=ALU.mult, op1=ALU.subtract).then_inc(neg_done, 1)
                        if slot == (3, 0):
                            dve.wait_ge(one_plus_done, k)
                            dve.reciprocal(score[:, :, :], one_plus[:, :, :]).then_inc(score_done, 1)
                        if slot in ((3, 1), (4, 1)):
                            chunk = slot[0] - 3
                            if chunk == 0:
                                dve.wait_ge(sel_done, k)
                            dve.wait_ge(silu_tanh_done, (k - 1) * SHARED + chunk + 1)
                            dve.scalar_tensor_tensor(out=silu_a[:, chunk, :], in0=silu_tanh[:, chunk, :], scalar=1.0,
                                                     in1=work[chunk][:, 0:GT], op0=ALU.add, op1=ALU.mult).then_inc(silu_a_done, 1)
                        if slot in ((4, 0), (5, 0)):
                            chunk = slot[0] - 4
                            if chunk == 0:
                                dve.wait_ge(top_done, k)
                            dve.wait_ge(silu_a_done, (k - 1) * SHARED + chunk + 1)
                            dve.tensor_tensor(hid_s[:, a, chunk, :], silu_a[:, chunk, :],
                                              work[chunk][:, GT:2 * GT], ALU.mult).then_inc(hid_s_done, 1)
                        if slot == (3, 1):
                            for tile in range(TILES):
                                ins = dve.max(top8[:, tile, :], sel_score[:, tile, :])
                            ins.then_inc(top_done, 1)
                        if slot == (4, 0):
                            for tile in range(TILES):
                                ins = dve.max_index(top8_at[:, tile, :], top8[:, tile, :], sel_score[:, tile, :])
                            ins.then_inc(top_at_done, 1)
                        if slot == (4, 1):
                            dve.wait_ge(top_at_done, k)
                            iota = small_sb[:, S_IOTA:S_END].rearrange("p (t e) -> p t e", e=E)
                            for n, pick in enumerate((first, second)):
                                ins = dve.tensor_tensor(pick[:, :, :], iota, top8_at[:, :, n:n + 1].broadcast_to([P, TILES, E]),
                                                        ALU.is_equal)
                            ins.then_inc(picked_done, 1)
                        if slot == (5, 1):
                            dve.wait_ge(chosen_done, k)
                            dve.reduce_sum(denom[:, :], chosen[:, :, :], AX_X).then_inc(denom_done, 1)
                        if slot == (6, 0):
                            dve.wait_ge(denom_eps_done, k)
                            dve.reciprocal(inverse[:, :], denom_eps[:, :]).then_inc(inverse_done, 1)
                            dve.tensor_scalar(even_gate[:, :], denom[:, :], EPS, 0.5, ALU.is_le, ALU.mult)
                            dve.wait_ge(inverse_done, k)
                            dve.scalar_tensor_tensor(out=gate_scale[:, :], in0=denom[:, :], scalar=EPS,
                                                     in1=inverse[:, :], op0=ALU.is_gt, op1=ALU.mult).then_inc(scale_done, 1)
                    if has_b(at) and slot == (7, 1):
                        dve.wait_ge(out_done, k - 1)
                        dve.wait_ge(out_free[b], (k - b) * 8)
                        dve.scalar_tensor_tensor(out=out_sb[:, b, :], in0=bank_o[:, 0:GT], scalar=1.0 / 3.0,
                                                 in1=x1[:, b, :], op0=ALU.mult, op1=ALU.add).then_inc(final_done, 1)

                for s in range(GS):
                    if has_steps(at):
                        t = k * GS + s
                        before = g_hist[:, parity, (s - 1) * B:s * B] if s else g_hist[:, 1 - parity, GT - B:GT]
                        if at == 0 and s == 0:
                            dve.wait_ge(g_init, 1)
                        else:
                            dve.wait_ge(g_done, t)
                        dve.wait_ge(r_ready, t + 1)
                        dve.scalar_tensor_tensor(out=reset[:, :], in0=tanh_r[:, :], scalar=1.0, in1=before,
                                                 op0=ALU.add, op1=ALU.mult).then_inc(reset_ready, 1)
                        dve.wait_ge(reset_ready, t * 3 + 1)
                        dve.tensor_tensor(reset_rest[:, :], reset[:, :], top_half(reset[:, :]), ALU.subtract).then_inc(reset_ready, 1)
                        dve.wait_ge(z_ready, t + 1)
                        dve.scalar_tensor_tensor(out=kept[:, :], in0=tanh_z[:, :], scalar=1.0, in1=before,
                                                 op0=ALU.add, op1=ALU.mult).then_inc(kept_ready, 1)
                        dve.wait_ge(reset_ready, t * 3 + 2)
                        dve.tensor_tensor(reset_low[:, :], reset_rest[:, :], top_half(reset_rest[:, :]), ALU.subtract).then_inc(reset_ready, 1)
                        dve.wait_ge(kept_ready, t * 3 + 1)
                        dve.tensor_tensor(kept_rest[:, :], kept[:, :], top_half(kept[:, :]), ALU.subtract).then_inc(kept_ready, 1)
                        dve.wait_ge(kept_ready, t * 3 + 2)
                        dve.tensor_tensor(kept_low[:, :], kept_rest[:, :], top_half(kept_rest[:, :]), ALU.subtract).then_inc(kept_ready, 1)
                    fill((s, 0))
                    if has_steps(at):
                        dve.wait_ge(cand_ready, t + 1)
                        dve.scalar_tensor_tensor(out=upd[:, :], in0=tanh_z[:, :], scalar=1.0, in1=cand[:, :],
                                                 op0=ALU.subtract, op1=ALU.mult).then_inc(upd_ready, 1)
                        dve.wait_ge(upd_ready, t * 3 + 1)
                        dve.tensor_tensor(upd_rest[:, :], upd[:, :], top_half(upd[:, :]), ALU.subtract).then_inc(upd_ready, 1)
                        dve.scalar_tensor_tensor(out=g_hist[:, parity, s * B:(s + 1) * B], in0=kept[:, :], scalar=0.5,
                                                 in1=upd[:, :], op0=ALU.mult, op1=ALU.subtract).then_inc(g_done, 1)
                        dve.wait_ge(upd_ready, t * 3 + 2)
                        dve.tensor_tensor(upd_low[:, :], upd_rest[:, :], top_half(upd_rest[:, :]), ALU.subtract).then_inc(upd_ready, 1)
                    if at == 0 and s == GS // 4:
                        experts_setup()
                    if at == 0 and s == GS - 2:
                        keep_cond_scores()
                    fill((s, 1))

            over_groups(dve, group)

        @block.gpsimd
        def _(pool):
            pool.memset(euler[:, :, :], EULER)
            pool.memset(unit[:, :, :], 1.0)
            pool.memset(epsilon[:, :], EPS).then_inc(constants_set, 1)
            pool.wait_ge(constants_set, 1)

            def group(k, parity, at):
                if not has_a(at):
                    return
                pool.wait_ge(neg_done, k)
                pool.tensor_tensor(exp_neg[:, :, :], euler[:, :, :], neg_logit[:, :, :], ALU.pow).then_inc(exp_done, 1)
                pool.wait_ge(exp_done, k)
                pool.tensor_tensor(one_plus[:, :, :], exp_neg[:, :, :], unit[:, :, :], ALU.add).then_inc(one_plus_done, 1)
                pool.wait_ge(score_done, k)
                rbias = small_sb[:, S_RBIAS:S_IOTA].rearrange("p (t e) -> p t e", e=E)
                pool.tensor_tensor(sel_score[:, :, :], score[:, :, :], rbias, ALU.add).then_inc(sel_done, 1)
                pool.wait_ge(picked_done, k)
                pool.tensor_tensor(mask[:, :, :], first[:, :, :], second[:, :, :], ALU.add).then_inc(mask_done, 1)
                pool.wait_ge(mask_done, k)
                pool.tensor_tensor(chosen[:, :, :], mask[:, :, :], score[:, :, :], ALU.mult).then_inc(chosen_done, 1)
                pool.wait_ge(denom_done, k)
                pool.tensor_tensor(denom_eps[:, :], denom[:, :], epsilon[:, :], ALU.add).then_inc(denom_eps_done, 1)
                pool.wait_ge(scale_done, k)
                for out, data, scale in ((by_score, chosen, gate_scale), (by_half, mask, even_gate)):
                    pool.tensor_tensor(out[:, :, :], data[:, :, :],
                                       scale[:, :].rearrange("p (t e) -> p t e", e=1).broadcast_to([P, TILES, E]),
                                       ALU.mult).then_inc(gated_done, 1)
                pool.wait_ge(gated_done, k * 2)
                pool.tensor_tensor(combine[:, :, :], by_score[:, :, :], by_half[:, :, :], ALU.add).then_inc(combine_done, 1)
                pool.wait_ge(combine_done, k)

                def top(t):
                    return t[:, :, :].bitcast(BF16)[:, :, 1::2]

                pool.tensor_tensor(comb_rest[:, :, :], combine[:, :, :], top(combine), ALU.subtract).then_inc(comb_rest_done, 1)
                pool.tensor_copy(comb_parts[:, :, 0, :], top(combine))
                pool.wait_ge(comb_rest_done, k)
                pool.tensor_tensor(comb_parts[:, :, 2, :], comb_rest[:, :, :], top(comb_rest), ALU.subtract)
                pool.tensor_copy(comb_parts[:, :, 1, :], top(comb_rest)).then_inc(parts_done, 1)

            over_groups(pool, group)


def kernel(x, cond_1024, L0_cond_Wxz, L0_cond_bxz, L0_cond_Whz, L0_cond_bhz, L0_cond_Wxr, L0_cond_bxr, L0_cond_Whr,
           L0_cond_bhr, L0_cond_Wxh, L0_cond_bxh, L0_cond_Whh, L0_cond_bhh, L0_cond_Whq, L0_cond_bhq,
           L1_cond_router_w, L1_cond_router_t_w, L1_cond_router_bias, L1_cond_sw1, L1_cond_sw3, L1_cond_sw2,
           L1_cond_rw1, L1_cond_rw2):
    import ml_dtypes
    import numpy as np
    import concourse.bacc as _bacc
    from concourse.bass_utils import run_bass_kernel_spmd as _run

    def arr(a):
        return np.asarray(a)

    def side_by_side(*parts):
        return np.ascontiguousarray(np.concatenate(parts, axis=1))

    rw1 = arr(L1_cond_rw1).reshape(E * 64, C).T
    sw2 = arr(L1_cond_sw2).T.reshape(SHARED, P, C).transpose(1, 0, 2).reshape(P, SHARED * C)
    rw2 = arr(L1_cond_rw2).transpose(0, 2, 1).reshape(PAIRS, P, C).transpose(1, 0, 2).reshape(P, PAIRS * C)
    iota = np.tile(np.arange(E, dtype=np.float32), (P, TILES))
    chunk_of = np.arange(P) // 64
    select = np.zeros((3, E, PAIRS, P), ml_dtypes.bfloat16)
    for pair in range(PAIRS):
        for e in range(2):
            select[:, 2 * pair + e, pair, chunk_of == e] = 1
    arrays = {
        "x_t": np.ascontiguousarray(arr(x).transpose(2, 1, 0).reshape(C, T * B)),
        "w_in": side_by_side(arr(L0_cond_Wxr).T, arr(L0_cond_Wxz).T, arr(L0_cond_Wxh).T),
        "w_rec": side_by_side(arr(L0_cond_Whr).T, arr(L0_cond_Whz).T, arr(L0_cond_Whh).T),
        "b_in": np.concatenate([arr(L0_cond_bxr), arr(L0_cond_bxz), arr(L0_cond_bxh)])[None, :],
        "b_rec": np.concatenate([arr(L0_cond_bhr), arr(L0_cond_bhz), arr(L0_cond_bhh)])[None, :],
        "w_moe": side_by_side(arr(L0_cond_Whq).T, arr(L1_cond_sw1).T, arr(L1_cond_sw3).T, rw1, sw2, rw2,
                              arr(L1_cond_router_w).T, arr(L1_cond_router_t_w).T),
        "small": side_by_side(np.tile(arr(cond_1024).T, (1, P // B)), arr(L0_cond_bhq)[:, None],
                              np.tile(arr(L1_cond_router_bias), (P, TILES)), iota),
        "selectors": select.reshape(3 * E, PAIRS, P),
        "identity": np.eye(P, dtype=ml_dtypes.bfloat16),
    }
    nc = _bacc.Bacc("TRN2", target_bir_lowering=False, num_devices=1)
    args = [nc.dram_tensor(name, a.shape, mybir.dt.from_np(a.dtype), kind="ExternalInput").ap()
            for name, a in arrays.items()]
    out_t = nc.dram_tensor("out_t", (C, T * B), F32, kind="ExternalOutput").ap()
    gru_moe_program(nc, *args, out_t)
    result = _run(nc, [arrays], core_ids=[0])
    return np.ascontiguousarray(np.asarray(result.results[0]["out_t"]).reshape(C, T, B).transpose(2, 1, 0))
```

```python
from contextlib import ExitStack

import concourse.bass as bass
from concourse import mybir

F32 = mybir.dt.float32
BF16 = mybir.dt.bfloat16
F32R = mybir.dt.float32r
F16 = mybir.dt.float16
U32 = mybir.dt.uint32
ALU = mybir.AluOpType
ACT = mybir.ActivationFunctionType
AX_X = mybir.AxisListType.X

P = 128
B, T, C, E = 32, 128, 128, 8
GS = 8
GT = GS * B
GROUPS = T // GS
TILES = GT // P
PAIR_BANK = (0, 1, 2, 2)
SHARED = 2
PAIRS = 4
WARM_UP = (28, 5)
PROJECT = ((5, 0), (6, 1), (7, 1))
READ_OUT, ROUTER, TURN_GATES = (0, 0), (1, 1), (7, 2)
SHARED_HIDDEN = ((2, 1), (2, 2), (3, 1), (3, 2))
ROUTED_HIDDEN = ((0, 1), (2, 0), (4, 0), (5, 1))
OUT_SHARED = ((1, 0), (1, 2))
OUT_ROUTED = ((3, 0), (4, 1), (6, 0), (7, 0))
A_SLOTS = (READ_OUT,) + SHARED_HIDDEN
IDLE_PRODUCTS = (3, 4)
HIDDEN_CUTS = 4
EPS = 1e-9
EULER = 2.718281828459045

W_Q = 0
W_SW1 = W_Q + C
W_SW3 = W_SW1 + SHARED * P
W_RW1 = W_SW3 + SHARED * P
W_SW2 = W_RW1 + PAIRS * P
W_RW2 = W_SW2 + SHARED * C
W_ROUTER = W_RW2 + PAIRS * C
W_ROUTER_T = W_ROUTER + E
W_END = W_ROUTER_T + E
S_COND = 0
S_BHQ = S_COND + P
S_RBIAS = S_BHQ + 1
S_IOTA = S_RBIAS + TILES * E
S_BIAS_IN = S_IOTA + TILES * E
S_BIAS_REC = S_BIAS_IN + 3
S_END = S_BIAS_REC + 3
R_KEPT, R_UPD, H_RESET, RW_END = (P * i for i in range(4))


def gru_moe_program(nc: bass.Bass, x_t, w_in, w_rec, w_moe, small, selectors, identity, gate_of_rows, out_t):
    with ExitStack() as ctx:
        def sb(name, shape, dtype=F32):
            return ctx.enter_context(nc.sbuf_tensor(name, shape, dtype))

        def sem(name):
            return ctx.enter_context(nc.semaphore(name))

        def bank(name):
            return ctx.enter_context(nc.psum_tensor(name, [P, 512], F32))

        x_ring = sb("x_ring", [P, 2, GT])
        w_in_sb = sb("w_in_sb", [P, 3 * P])
        w_rec_sb = sb("w_rec_sb", [P, 3 * P])
        w_scaled = sb("w_scaled", [P, RW_END])
        z_whole = sb("z_whole", [P, P])
        z_rest = sb("z_rest", [P, P])
        z_split = sb("z_split", [P, 3, P], BF16)
        moe_w = sb("moe_w", [P, W_END])
        small_sb = sb("small_sb", [P, S_END])
        sel_sb = sb("sel_sb", [3 * E, PAIRS, P], BF16)
        ident = sb("ident", [P, P], BF16)
        bias_sum = sb("bias_sum", [P, 3])
        bias_rest = sb("bias_rest", [P, 3])
        bias_part = sb("bias_part", [P, 3, 3], BF16)
        bias_t = sb("bias_t", [9, P], BF16)
        gate_rows = sb("gate_rows", [9, 3, GT], BF16)
        zeros = sb("zeros", [P, GT], BF16)
        table_out = sb("table_out", [P, 1])
        tanh_r = sb("tanh_r", [P, B])
        tanh_z = sb("tanh_z", [P, B])
        cand = sb("cand", [P, B])
        reset = sb("reset", [P, B])
        kept = sb("kept", [P, B])
        upd = sb("upd", [P, B])
        state_high = sb("state_high", [P, B], F16)
        state_low = sb("state_low", [P, B], F16)
        g_hist = sb("g_hist", [P, 2, GT])
        x1 = sb("x1", [P, 2, GT])
        x1_high = sb("x1_high", [P, 2, GT], F32R)
        x1_low = sb("x1_low", [P, 2, GT], F32R)
        hidden_high = sb("hidden_high", [P, W_SW2 - W_SW1], F32R)
        hidden_low = sb("hidden_low", [P, W_SW2 - W_SW1], F32R)
        silu_tanh = sb("silu_tanh", [P, SHARED, GT])
        silu_a = sb("silu_a", [P, SHARED, GT])
        hid_s = sb("hid_s", [P, 2, SHARED, GT])
        gelu = sb("gelu", [P, PAIRS, GT])
        hid_r = sb("hid_r", [P, PAIRS, GT])
        out_sb = sb("out_sb", [P, 2, GT])
        t_bias = sb("t_bias", [P, TILES, E])
        euler = sb("euler", [P, TILES, E])
        unit = sb("unit", [P, TILES, E])
        epsilon = sb("epsilon", [P, TILES])
        neg_logit = sb("neg_logit", [P, TILES, E])
        exp_neg = sb("exp_neg", [P, TILES, E])
        one_plus = sb("one_plus", [P, TILES, E])
        score = sb("score", [P, TILES, E])
        sel_score = sb("sel_score", [P, TILES, E])
        top8 = sb("top8", [P, TILES, 8])
        top8_at = sb("top8_at", [P, TILES, 8], U32)
        first = sb("first", [P, TILES, E])
        second = sb("second", [P, TILES, E])
        mask = sb("mask", [P, TILES, E])
        chosen = sb("chosen", [P, TILES, E])
        denom = sb("denom", [P, TILES])
        denom_eps = sb("denom_eps", [P, TILES])
        inverse = sb("inverse", [P, TILES])
        gate_scale = sb("gate_scale", [P, TILES])
        even_gate = sb("even_gate", [P, TILES])
        by_score = sb("by_score", [P, TILES, E])
        by_half = sb("by_half", [P, TILES, E])
        combine = sb("combine", [P, TILES, E])
        comb_rest = sb("comb_rest", [P, TILES, E])
        comb_parts = sb("comb_parts", [P, TILES, 3, E], BF16)
        comb_t = sb("comb_t", [3 * E, GT], BF16)

        bank_r, bank_z, bank_h = bank("bank_r"), bank("bank_z"), bank("bank_h")
        work = [bank("work0"), bank("work1"), bank("work2")]
        bank_o = bank("bank_o")
        bank_m = bank("bank_m")
        y_ps = bank_m[:, 0:GT]
        score_ps = bank_m[:, GT:GT + TILES * E]
        bias_ps = bank_m[0:9, 384:384 + P // 2].bitcast(BF16)
        comb_ps = bank_o[0:3 * E, GT:GT + GT // 2].bitcast(BF16)
        late_comb_ps = bank_m[0:3 * E, 384:384 + GT // 2].bitcast(BF16)

        small_loaded, w_in_loaded, w_rec_loaded, moe_loaded = sem("small_loaded"), sem("w_in_loaded"), sem("w_rec_loaded"), sem("moe_loaded")
        x_loaded, out_free = [sem("x_loaded0"), sem("x_loaded1")], [sem("out_free0"), sem("out_free1")]
        setup_step, z_setup_step, zeroed, bias_split, bias_turned, bias_ready = sem("setup_step"), sem("z_setup_step"), sem("zeroed"), sem("bias_split"), sem("bias_turned"), sem("bias_ready")
        w_reset_ready, w_gates_ready, w_z_ready = sem("w_reset_ready"), sem("w_gates_ready"), sem("w_z_ready")
        g_init, tb_ps_done, table_ready, moe_scaled = sem("g_init"), sem("tb_ps_done"), sem("table_ready"), sem("moe_scaled")
        r_pre, z_pre, h_pre = sem("r_pre"), sem("z_pre"), sem("h_pre")
        r_ready, z_ready, cand_ready = sem("r_ready"), sem("z_ready"), sem("cand_ready")
        reset_ready, kept_ready, upd_ready = sem("reset_ready"), sem("kept_ready"), sem("upd_ready")
        state_split = sem("state_split")
        half_zeroed = sem("half_zeroed")
        g_done = sem("g_done")
        y_done, scores_done, comb_t_done = sem("y_done"), sem("scores_done"), sem("comb_t_done")
        silu_pre, gelu_pre, out_done = sem("silu_pre"), sem("gelu_pre"), sem("out_done")
        silu_tanh_done, gelu_done, comb_copied = sem("silu_tanh_done"), sem("gelu_done"), sem("comb_copied")
        x1_high_done, x1_low_done = sem("x1_high_done"), sem("x1_low_done")
        hidden_high_done, hidden_split = sem("hidden_high_done"), sem("hidden_split")
        x1_done, silu_a_done, hid_s_done, hid_r_done = sem("x1_done"), sem("silu_a_done"), sem("hid_s_done"), sem("hid_r_done")
        final_done, late_gates_done = sem("final_done"), sem("late_gates_done")
        neg_done, score_done, top_done, top_at_done = sem("neg_done"), sem("score_done"), sem("top_done"), sem("top_at_done")
        picked_done, denom_done, inverse_done, scale_done = sem("picked_done"), sem("denom_done"), sem("inverse_done"), sem("scale_done")
        exp_done, one_plus_done, sel_done = sem("exp_done"), sem("one_plus_done"), sem("sel_done")
        constants_set, mask_done, denom_eps_done = sem("constants_set"), sem("mask_done"), sem("denom_eps_done")
        gated_done, combine_done, comb_rest_done, parts_done = sem("gated_done"), sem("combine_done"), sem("comb_rest_done"), sem("parts_done")

        def over_groups(eng, group):
            group(0, 0, 0)
            group(1, 1, 1)
            with eng.Fori(0, (GROUPS - 4) // 4) as quad:
                for n in range(4):
                    group(quad * 4 + (2 + n), n % 2, None)
            group(GROUPS - 2, 0, GROUPS - 2)
            group(GROUPS - 1, 1, GROUPS - 1)

        def has_next(at):
            return at is None or at < GROUPS - 1

        def has_a(at):
            return at is None or at >= 1

        def has_b(at):
            return at is None or at >= 2

        def hidden_cut(n):
            width = (W_SW2 - W_SW1) // HIDDEN_CUTS
            return n * width, (n + 1) * width

        def tail_bank(pair):
            return bank_h if pair == 3 else work[PAIR_BANK[pair]]

        def late_hidden(pair):
            return (bank_r, bank_z)[pair // 2][:, pair % 2 * GT:(pair % 2 + 1) * GT]

        def late_gate(pair):
            return (work[0], work[1], work[2], bank_h)[pair][:, 0:GT]

        block = ctx.enter_context(nc.Block())

        @block.sync
        def _(sp):
            for half in out_free:
                sp.sem_inc(half, 16)
            sp.dma_start(x_ring[:, 0, :], x_t[:, 0:GT]).then_inc(x_loaded[0], 16)
            sp.dma_start(w_in_sb[:, :], w_in).then_inc(w_in_loaded, 16)
            sp.dma_start(x_ring[:, 1, :], x_t[:, GT:2 * GT]).then_inc(x_loaded[1], 16)
            sp.dma_start(moe_w[:, :], w_moe).then_inc(moe_loaded, 16)
            sp.dma_start(sel_sb[:, :, :], selectors).then_inc(moe_loaded, 16)

            def store(k, parity):
                sp.wait_ge(final_done, k - 1)
                sp.dma_start(out_t[:, bass.ds((k - 2) * GT, GT)], out_sb[:, parity, :]).then_inc(out_free[parity], 16)

            def group(k, parity, at):
                if has_a(at) and has_next(at):
                    sp.wait_ge(x1_done, k)
                    sp.dma_start(x_ring[:, 1 - parity, :],
                                 x_t[:, bass.ds((k + 1) * GT, GT)]).then_inc(x_loaded[1 - parity], 16)
                if has_b(at):
                    store(k, parity)

            over_groups(sp, group)
            store(GROUPS, 0)
            store(GROUPS + 1, 1)
            for half in out_free:
                sp.wait_ge(half, 16 + 16 * GROUPS // 2)

        @block.tensor
        def _(pe):
            def recur(dst, col, weights, data):
                return pe.matmul(dst[:, col:col + B], w_scaled[:, weights:weights + P], data[:, :],
                                 start=False, stop=True, skip_group_check=True)

            def recur_z(col, data, part):
                for m in range(3 - part):
                    last = pe.matmul(bank_z[:, col:col + B], z_split[:, m, :], data[:, :],
                                     start=False, stop=True, skip_group_check=True)
                return last

            def project(dst, gate, parity, start=False):
                half = dst[:, parity * GT:(parity + 1) * GT]
                pe.matmul(half, w_in_sb[:, gate * P:(gate + 1) * P], x_ring[:, parity, :],
                          start=start, stop=True, skip_group_check=True)
                pe.matmul(half, bias_t[:, :], gate_rows[:, gate, :],
                          start=False, stop=True, skip_group_check=True)

            def keep_warm(n, dst=bank_o[:, 0:GT], start=True):
                for _ in range(n):
                    pe.matmul(dst, zeros[:, 0:P], zeros[:, :], start=start, stop=True, skip_group_check=True)

            def weights(col, width=P):
                return moe_w[:, col:col + width]

            def hidden(dst, col, half):
                col -= W_SW1
                for n, (w, x) in enumerate(((hidden_high, x1_high), (hidden_low, x1_high), (hidden_high, x1_low))):
                    last = pe.matmul(dst, w[:, col:col + P], x[:, half, :], start=(n == 0), stop=(n == 2))
                return last

            def read_out(k, a):
                pe.wait_ge(g_done, k * GS)
                pe.matmul(y_ps, weights(W_Q), g_hist[:, a, :], start=True, stop=True).then_inc(y_done, 1)

            def router(k, a, tile):
                if tile == 0:
                    pe.wait_ge(x1_done, k)
                mm = pe.matmul(score_ps[:, tile * E:(tile + 1) * E], x1[:, a, tile * P:(tile + 1) * P],
                               weights(W_ROUTER, E), start=True, stop=True)
                if tile == TILES - 1:
                    mm.then_inc(scores_done, 1)

            def shared_hidden(k, a, chunk, with_b, half):
                dst = work[chunk]
                if half == 0:
                    if chunk == 0:
                        pe.wait_ge(x1_low_done, k)
                    if with_b:
                        pe.wait_ge(hid_r_done, (k - 2) * PAIRS + chunk + 1)
                    hidden(dst[:, 0:GT], W_SW1 + chunk * P, a)
                else:
                    hidden(dst[:, GT:2 * GT], W_SW3 + chunk * P, a).then_inc(silu_pre, 1)

            def routed_hidden(k, b, pair, dst=None):
                if pair == 0:
                    pe.wait_ge(comb_copied, k - 1)
                    pe.wait_ge(hid_s_done, (k - 2) * SHARED + 1)
                elif pair == 1:
                    pe.wait_ge(hid_s_done, (k - 1) * SHARED)
                elif pair == 3 and dst is None:
                    pe.wait_ge(hid_r_done, (k - 2) * PAIRS + 3)
                dst = dst or work[PAIR_BANK[pair]]
                pe.matmul(dst[:, GT:2 * GT], sel_sb[:, pair, :], comb_t[:, :], start=True, stop=True)
                hidden(dst[:, 0:GT], W_RW1 + pair * P, b).then_inc(gelu_pre, 1)

            def out_shared(k, b, chunk):
                pe.matmul(bank_o[:, 0:GT], weights(W_SW2 + chunk * C), hid_s[:, b, chunk, :],
                          start=(chunk == 0), stop=False)

            def out_routed(k, pair):
                pe.wait_ge(hid_r_done, (k - 2) * PAIRS + pair + 1)
                mm = pe.matmul(bank_o[:, 0:GT], weights(W_RW2 + pair * C), hid_r[:, pair, :],
                               start=False, stop=(pair == PAIRS - 1))
                if pair == PAIRS - 1:
                    mm.then_inc(out_done, 1)

            def turn_gates(k, dst):
                pe.wait_ge(parts_done, k)
                for tile in range(TILES):
                    mm = pe.transpose(dst[:, tile * P:(tile + 1) * P],
                                      comb_parts[:, tile, :, :].rearrange("p m e -> p (m e)"), ident[:, :])
                mm.then_inc(comb_t_done, 1)

            pe.wait_ge(zeroed, 1)
            keep_warm(WARM_UP[0])
            pe.wait_ge(bias_split, 1)
            pe.transpose(bias_ps, bias_part[:, :, :].rearrange("p m g -> p (m g)"), ident[:, :]).then_inc(bias_turned, 1)
            keep_warm(WARM_UP[1])
            pe.wait_ge(x_loaded[0], 16)
            pe.wait_ge(w_in_loaded, 16)
            pe.wait_ge(w_rec_loaded, 16)
            pe.wait_ge(bias_ready, 1)
            cond = small_sb[:, S_COND:S_COND + B]
            project(bank_r, 0, 0, start=True)
            pe.matmul(bank_r[:, 0:B], w_rec_sb[:, 0:P], cond,
                      start=False, stop=True, skip_group_check=True).then_inc(r_pre, 1)
            project(bank_z, 1, 0, start=True)
            pe.matmul(bank_z[:, 0:B], w_rec_sb[:, P:2 * P], cond,
                      start=False, stop=True, skip_group_check=True).then_inc(z_pre, 1)
            project(bank_h, 2, 0, start=True)
            pe.wait_ge(w_reset_ready, 1)

            def group(k, parity, at):
                a, b = 1 - parity, parity

                def fill(slot):
                    if has_next(at):
                        if slot == PROJECT[0]:
                            pe.wait_ge(x_loaded[1 - parity], x_count(k, parity))
                        if slot in PROJECT:
                            gate = PROJECT.index(slot)
                            if has_a(at):
                                pe.wait_ge(half_zeroed, (k - 1) * 3 + gate + 1)
                            project((bank_r, bank_z, bank_h)[gate], gate, 1 - parity)
                    elif slot in PROJECT:
                        if slot == PROJECT[2]:
                            pe.wait_ge(cand_ready, k * GS + GS)
                        keep_warm(5, (bank_r, bank_z, bank_h)[PROJECT.index(slot)][:, 0:GT], start=False)
                    if has_a(at):
                        if slot == READ_OUT:
                            read_out(k, a)
                        if slot == ROUTER:
                            router(k, a, 0)
                            router(k, a, 1)
                        if slot in SHARED_HIDDEN:
                            n = SHARED_HIDDEN.index(slot)
                            shared_hidden(k, a, n // 2, has_b(at), n % 2)
                    if has_b(at):
                        if slot in OUT_SHARED:
                            out_shared(k, b, OUT_SHARED.index(slot))
                        if slot in OUT_ROUTED:
                            out_routed(k, OUT_ROUTED.index(slot))
                        if slot in ROUTED_HIDDEN:
                            routed_hidden(k, b, ROUTED_HIDDEN.index(slot))
                    elif slot[1] < 2 and not (has_a(at) and slot in A_SLOTS) and slot not in PROJECT:
                        keep_warm(IDLE_PRODUCTS[slot[1]])
                    if not has_next(at) and slot == TURN_GATES:
                        read_out(GROUPS, parity)
                    if has_a(at) and slot == TURN_GATES:
                        if has_b(at):
                            pe.wait_ge(final_done, k - 1)
                        turn_gates(k, comb_ps)

                if at == 1:
                    pe.wait_ge(hidden_split, HIDDEN_CUTS)

                for s in range(GS):
                    here = parity * GT + s * B
                    nxt = here + B if s < GS - 1 else (1 - parity) * GT
                    pe.wait_ge(reset_ready, k * GS + s + 1)
                    recur(bank_h, here, H_RESET, reset).then_inc(h_pre, 1)
                    if at == 0 and s == 0:
                        pe.wait_ge(w_gates_ready, 1)
                    if at == 0 and s == GS // 2:
                        pe.wait_ge(moe_scaled, 1)
                        pe.matmul(score_ps[:, 0:E], small_sb[:, S_COND:S_COND + P], weights(W_ROUTER_T, E),
                                  start=True, stop=True).then_inc(tb_ps_done, 1)
                    fill((s, 0))
                    if has_next(at) or s < GS - 1:
                        pe.wait_ge(kept_ready, k * GS + s + 1)
                        recur(bank_r, nxt, R_KEPT, kept)
                        pe.wait_ge(upd_ready, k * GS + s + 1)
                        recur(bank_r, nxt, R_UPD, upd).then_inc(r_pre, 1)
                    fill((s, 1))
                    if has_next(at) or s < GS - 1:
                        if at == 0 and s == 0:
                            pe.wait_ge(w_z_ready, 1)
                        if has_a(at) and has_next(at) and s == 5:
                            pe.wait_ge(half_zeroed, (k - 1) * 3 + 2)
                        for part, data in enumerate((state_high, state_low)):
                            pe.wait_ge(state_split, (k * GS + s) * 2 + part + 1)
                            mm = recur_z(nxt, data, part)
                        mm.then_inc(z_pre, 1)
                    fill((s, 2))

            def x_count(k, parity):
                return (k + 1 - (1 - parity)) * 8 + 16

            over_groups(pe, group)

            k, a, b = GROUPS, 1, 0
            routed_hidden(k, b, 0)
            router(k, a, 0)
            router(k, a, 1)
            routed_hidden(k, b, 1)
            pe.wait_ge(final_done, k - 2)
            out_shared(k, b, 0)
            routed_hidden(k, b, 2)
            out_shared(k, b, 1)
            routed_hidden(k, b, 3, tail_bank(3))
            for chunk in range(SHARED):
                shared_hidden(k, a, chunk, True, 0)
                shared_hidden(k, a, chunk, True, 1)
            for pair in range(PAIRS):
                out_routed(k, pair)
                mm = hidden(late_hidden(pair), W_RW1 + pair * P, a)
                if pair % 2:
                    mm.then_inc(gelu_pre, 2)
            pe.wait_ge(final_done, k - 1)
            pe.wait_ge(hid_s_done, k * SHARED)
            out_shared(k + 1, a, 0)
            out_shared(k + 1, a, 1)
            turn_gates(k, late_comb_ps)
            keep_warm(6, bank_h[:, 0:GT], start=False)
            pe.wait_ge(comb_copied, k)
            for pair in range(PAIRS):
                pe.matmul(late_gate(pair), sel_sb[:, pair, :], comb_t[:, :], start=True, stop=True).then_inc(late_gates_done, 1)
            for pair in range(PAIRS):
                out_routed(k + 1, pair)

        @block.scalar
        def _(act):
            act.dma_start(small_sb[:, :], small).then_inc(small_loaded, 16)
            act.dma_start(ident[:, :], identity).then_inc(small_loaded, 16)
            act.dma_start(w_rec_sb[:, :], w_rec).then_inc(w_rec_loaded, 16)
            act.dma_start(gate_rows[:, :, :], gate_of_rows).then_inc(small_loaded, 16)
            act.wait_ge(zeroed, 1)
            act.activation(table_out[:, :], zeros[:, 0:1], ACT.Gelu).then_inc(table_ready, 1)

            def silu_gate(k, chunk):
                act.wait_ge(silu_pre, (k - 1) * SHARED + chunk + 1)
                act.activation(silu_tanh[:, chunk, :], work[chunk][:, 0:GT], ACT.Tanh, scale=0.5).then_inc(silu_tanh_done, 1)

            def gelu_of(k, pair, src):
                act.wait_ge(gelu_pre, (k - 2) * PAIRS + pair + 1)
                act.activation(gelu[:, pair, :], src, ACT.Gelu).then_inc(gelu_done, 1)

            def keep_gates(k, src):
                act.wait_ge(comb_t_done, k - 1)
                act.activation(comb_t[:, :], src, ACT.Copy).then_inc(comb_copied, 1)

            def round_x1(k, a):
                act.wait_ge(x1_done, k)
                act.activation(x1_high[:, a, :], x1[:, a, :], ACT.Copy).then_inc(x1_high_done, 1)

            def zero_half(dst, parity):
                act.activation(dst[:, parity * GT:(parity + 1) * GT], zeros[:, :], ACT.Copy).then_inc(half_zeroed, 1)

            def group(k, parity, at):
                for s in range(GS):
                    col = parity * GT + s * B
                    act.wait_ge(r_pre, k * GS + s + 1)
                    act.activation(tanh_r[:, :], bank_r[:, col:col + B], ACT.Tanh, scale=0.5).then_inc(r_ready, 1)
                    if has_a(at) and has_next(at) and s == 4:
                        zero_half(bank_r, 1 - parity)
                    act.wait_ge(z_pre, k * GS + s + 1)
                    act.activation(tanh_z[:, :], bank_z[:, col:col + B], ACT.Tanh, scale=0.5).then_inc(z_ready, 1)
                    act.wait_ge(h_pre, k * GS + s + 1)
                    act.activation(cand[:, :], bank_h[:, col:col + B], ACT.Tanh).then_inc(cand_ready, 1)
                    if has_b(at) and s == 0:
                        keep_gates(k, comb_ps)
                    if has_a(at) and has_next(at) and s in (5, 7):
                        zero_half(bank_z if s == 5 else bank_h, 1 - parity)
                    if has_a(at) and s in (3, 4):
                        silu_gate(k, s - 3)
                    if has_a(at) and s == 1:
                        round_x1(k, 1 - parity)
                    if at == 0 and 3 <= s < 3 + HIDDEN_CUTS:
                        if s == 3:
                            act.wait_ge(moe_loaded, 32)
                        lo, hi = hidden_cut(s - 3)
                        act.activation(hidden_high[:, lo:hi], moe_w[:, W_SW1 + lo:W_SW1 + hi], ACT.Copy).then_inc(hidden_high_done, 1)
                    if has_b(at) and s in (1, 2, 4, 6):
                        pair = (1, 2, 4, 6).index(s)
                        gelu_of(k, pair, work[PAIR_BANK[pair]][:, 0:GT])

            over_groups(act, group)
            k = GROUPS
            keep_gates(k, comb_ps)
            round_x1(k, 1)
            for pair in range(PAIRS):
                gelu_of(k, pair, tail_bank(pair)[:, 0:GT])
            for chunk in range(SHARED):
                silu_gate(k, chunk)
            for pair in range(PAIRS):
                gelu_of(k + 1, pair, late_hidden(pair))
            keep_gates(k + 1, late_comb_ps)

        @block.vector
        def _(dve):
            done = [0]

            def then(ins):
                done[0] += 1
                ins.then_inc(setup_step, 1)
                dve.wait_ge(setup_step, done[0])

            dve.memset(zeros[:, :], 0.0).then_inc(zeroed, 1)
            dve.wait_ge(small_loaded, 48)
            then(dve.tensor_tensor(bias_sum[:, :], small_sb[:, S_BIAS_IN:S_BIAS_REC], small_sb[:, S_BIAS_REC:S_END], ALU.add))
            then(dve.tensor_copy(bias_part[:, 0, :], bias_sum[:, :]))
            then(dve.tensor_tensor(bias_rest[:, :], bias_sum[:, :], bias_part[:, 0, :], ALU.subtract))
            then(dve.tensor_copy(bias_part[:, 1, :], bias_rest[:, :]))
            dve.tensor_tensor(bias_part[:, 2, :], bias_rest[:, :], bias_part[:, 1, :], ALU.subtract).then_inc(bias_split, 1)
            dve.tensor_scalar(g_hist[:, 1, GT - B:GT], small_sb[:, S_COND:S_COND + B], 2.0, None, ALU.mult).then_inc(g_init, 1)
            def scale_weights(dst, gate, factor):
                return dve.tensor_scalar(w_scaled[:, dst:dst + P], w_rec_sb[:, gate * P:(gate + 1) * P], factor, None, ALU.mult)

            dve.wait_ge(w_rec_loaded, 16)
            scale_weights(H_RESET, 2, 0.25).then_inc(w_reset_ready, 1)

            scale_weights(R_KEPT, 0, 0.25)
            scale_weights(R_UPD, 0, -0.5).then_inc(w_gates_ready, 1)

            dve.wait_ge(bias_turned, 1)
            dve.tensor_copy(bias_t[:, :], bias_ps).then_inc(bias_ready, 1)

            def experts_setup():
                dve.wait_ge(moe_loaded, 32)
                then(dve.tensor_scalar(moe_w[:, W_Q:W_Q + C], moe_w[:, W_Q:W_Q + C], 0.5, None, ALU.mult))
                dve.tensor_scalar(moe_w[:, W_SW2:W_RW2], moe_w[:, W_SW2:W_RW2], 0.5, None, ALU.mult).then_inc(moe_scaled, 1)

            def keep_cond_scores():
                dve.wait_ge(tb_ps_done, 1)
                for tile in range(TILES):
                    ins = dve.tensor_copy(t_bias[:, tile, :], score_ps[:, 0:E])
                then(ins)

            def residual(k, a):
                dve.wait_ge(y_done, k)
                dve.scalar_tensor_tensor(out=x1[:, a, :], in0=y_ps, scalar=small_sb[:, S_BHQ:S_BHQ + 1],
                                         in1=x_ring[:, a, :], op0=ALU.add, op1=ALU.add).then_inc(x1_done, 1)

            def rest_of_x1(k, a):
                dve.wait_ge(x1_high_done, k)
                dve.tensor_tensor(x1_low[:, a, :], x1[:, a, :], x1_high[:, a, :].bitcast(F32), ALU.subtract).then_inc(x1_low_done, 1)

            def negate_logits(k):
                dve.wait_ge(scores_done, k)
                dve.scalar_tensor_tensor(out=neg_logit[:, :, :], in0=score_ps.rearrange("p (t e) -> p t e", e=E), scalar=-1.0,
                                         in1=t_bias[:, :, :], op0=ALU.mult, op1=ALU.subtract).then_inc(neg_done, 1)

            def sigmoid_scores(k):
                dve.wait_ge(one_plus_done, k)
                dve.reciprocal(score[:, :, :], one_plus[:, :, :]).then_inc(score_done, 1)

            def sort_scores():
                for tile in range(TILES):
                    ins = dve.max(top8[:, tile, :], sel_score[:, tile, :])
                ins.then_inc(top_done, 1)

            def sorted_experts():
                for tile in range(TILES):
                    ins = dve.max_index(top8_at[:, tile, :], top8[:, tile, :], sel_score[:, tile, :])
                ins.then_inc(top_at_done, 1)

            def pick_two(k):
                dve.wait_ge(top_at_done, k)
                iota = small_sb[:, S_IOTA:S_BIAS_IN].rearrange("p (t e) -> p t e", e=E)
                for n, pick in enumerate((first, second)):
                    ins = dve.tensor_tensor(pick[:, :, :], iota, top8_at[:, :, n:n + 1].broadcast_to([P, TILES, E]), ALU.is_equal)
                ins.then_inc(picked_done, 1)

            def sum_chosen(k):
                dve.wait_ge(mask_done, k)
                for tile in range(TILES):
                    ins = dve.tensor_tensor_reduce(chosen[:, tile, :], mask[:, tile, :], score[:, tile, :], 1.0, 0.0,
                                                   ALU.mult, ALU.add, denom[:, tile:tile + 1])
                ins.then_inc(denom_done, 1)

            def invert_sum(k):
                dve.wait_ge(denom_eps_done, k)
                dve.reciprocal(inverse[:, :], denom_eps[:, :]).then_inc(inverse_done, 1)
                dve.tensor_scalar(even_gate[:, :], denom[:, :], EPS, 0.5, ALU.is_le, ALU.mult)

            def scale_gates(k):
                dve.wait_ge(inverse_done, k)
                dve.scalar_tensor_tensor(out=gate_scale[:, :], in0=denom[:, :], scalar=EPS,
                                         in1=inverse[:, :], op0=ALU.is_gt, op1=ALU.mult).then_inc(scale_done, 1)

            def silu_first(k, chunk):
                dve.wait_ge(silu_tanh_done, (k - 1) * SHARED + chunk + 1)
                dve.scalar_tensor_tensor(out=silu_a[:, chunk, :], in0=silu_tanh[:, chunk, :], scalar=1.0,
                                         in1=work[chunk][:, 0:GT], op0=ALU.add, op1=ALU.mult).then_inc(silu_a_done, 1)

            def silu_second(k, a, chunk):
                dve.wait_ge(silu_a_done, (k - 1) * SHARED + chunk + 1)
                dve.tensor_tensor(hid_s[:, a, chunk, :], silu_a[:, chunk, :],
                                  work[chunk][:, GT:2 * GT], ALU.mult).then_inc(hid_s_done, 1)

            def gate_hidden(k, pair, gate):
                dve.wait_ge(gelu_done, (k - 2) * PAIRS + pair + 1)
                dve.tensor_tensor(hid_r[:, pair, :], gelu[:, pair, :], gate, ALU.mult).then_inc(hid_r_done, 1)

            def finish(k, b):
                dve.wait_ge(out_done, k - 1)
                dve.wait_ge(out_free[b], (k - b) * 8)
                dve.scalar_tensor_tensor(out=out_sb[:, b, :], in0=bank_o[:, 0:GT], scalar=1.0 / 3.0,
                                         in1=x1[:, b, :], op0=ALU.mult, op1=ALU.add).then_inc(final_done, 1)

            def group(k, parity, at):
                a, b = 1 - parity, parity

                def fill(slot):
                    if has_b(at) and slot == (0, 0):
                        silu_second(k - 1, b, 1)
                    if has_a(at):
                        if slot == (1, 0):
                            residual(k, a)
                        if slot == (1, 2):
                            rest_of_x1(k, a)
                        if slot == (2, 0):
                            negate_logits(k)
                        if slot == (4, 0):
                            silu_first(k, 0)
                            sigmoid_scores(k)
                        if slot == (4, 1):
                            dve.wait_ge(sel_done, k)
                        if slot == (4, 2):
                            sort_scores()
                        if slot == (5, 0):
                            dve.wait_ge(top_done, k)
                        if slot == (5, 1):
                            sorted_experts()
                        if slot == (5, 2):
                            pick_two(k)
                        if slot == (6, 0):
                            silu_first(k, 1)
                        if slot == (6, 1):
                            sum_chosen(k)
                        if slot == (7, 0):
                            invert_sum(k)
                            scale_gates(k)
                            silu_second(k, a, 0)
                    pair = {(2, 0): 0, (3, 0): 1, (5, 0): 2, (6, 2): 3}.get(slot)
                    if has_b(at) and pair is not None:
                        gate_hidden(k, pair, work[PAIR_BANK[pair]][:, GT:2 * GT])
                    if has_b(at) and slot == (7, 2):
                        finish(k, b)

                for s in range(GS):
                    t = k * GS + s
                    before = g_hist[:, parity, (s - 1) * B:s * B] if s else g_hist[:, 1 - parity, GT - B:GT]
                    if at == 0 and s == 0:
                        dve.wait_ge(g_init, 1)
                    else:
                        dve.wait_ge(g_done, t)
                    dve.wait_ge(r_ready, t + 1)
                    dve.scalar_tensor_tensor(out=reset[:, :], in0=tanh_r[:, :], scalar=1.0, in1=before,
                                             op0=ALU.add, op1=ALU.mult).then_inc(reset_ready, 1)
                    fill((s, 0))
                    dve.wait_ge(z_ready, t + 1)
                    dve.scalar_tensor_tensor(out=kept[:, :], in0=tanh_z[:, :], scalar=1.0, in1=before,
                                             op0=ALU.add, op1=ALU.mult).then_inc(kept_ready, 1)
                    fill((s, 1))
                    dve.wait_ge(cand_ready, t + 1)
                    dve.scalar_tensor_tensor(out=upd[:, :], in0=tanh_z[:, :], scalar=1.0, in1=cand[:, :],
                                             op0=ALU.subtract, op1=ALU.mult).then_inc(upd_ready, 1)
                    state = g_hist[:, parity, s * B:(s + 1) * B]
                    dve.wait_ge(upd_ready, t + 1)
                    dve.scalar_tensor_tensor(out=state, in0=kept[:, :], scalar=0.5,
                                             in1=upd[:, :], op0=ALU.mult, op1=ALU.subtract).then_inc(g_done, 1)
                    dve.scalar_tensor_tensor(out=state_high[:, :], in0=kept[:, :], scalar=0.5,
                                             in1=upd[:, :], op0=ALU.mult, op1=ALU.subtract).then_inc(state_split, 1)
                    dve.wait_ge(state_split, t * 2 + 1)
                    dve.tensor_tensor(state_low[:, :], state, state_high[:, :], ALU.subtract).then_inc(state_split, 1)
                    if at == 0 and 4 <= s < 4 + HIDDEN_CUTS:
                        dve.wait_ge(hidden_high_done, s - 3)
                        lo, hi = hidden_cut(s - 4)
                        dve.tensor_tensor(hidden_low[:, lo:hi], moe_w[:, W_SW1 + lo:W_SW1 + hi],
                                          hidden_high[:, lo:hi].bitcast(F32), ALU.subtract).then_inc(hidden_split, 1)
                    if at == 0 and s == GS // 4:
                        experts_setup()
                    if at == 0 and s == GS - 2:
                        keep_cond_scores()
                    fill((s, 2))

            over_groups(dve, group)

            k, a, b = GROUPS, 1, 0
            dve.wait_ge(final_done, k - 2)
            residual(k, a)
            silu_second(k - 1, b, 1)
            rest_of_x1(k, a)
            negate_logits(k)
            for pair in range(PAIRS):
                gate_hidden(k, pair, tail_bank(pair)[:, GT:2 * GT])
            sigmoid_scores(k)
            silu_first(k, 0)
            dve.wait_ge(sel_done, k)
            sort_scores()
            dve.wait_ge(top_done, k)
            sorted_experts()
            silu_first(k, 1)
            pick_two(k)
            silu_second(k, a, 0)
            sum_chosen(k)
            silu_second(k, a, 1)
            invert_sum(k)
            scale_gates(k)
            finish(k, b)
            for pair in range(PAIRS):
                dve.wait_ge(late_gates_done, pair + 1)
                gate_hidden(k + 1, pair, late_gate(pair))
            finish(k + 1, a)

        @block.gpsimd
        def _(pool):
            pool.memset(euler[:, :, :], EULER)
            pool.memset(unit[:, :, :], 1.0)
            pool.memset(epsilon[:, :], EPS).then_inc(constants_set, 1)
            pool.wait_ge(constants_set, 1)
            done = [0]

            def then(ins):
                done[0] += 1
                ins.then_inc(z_setup_step, 1)
                pool.wait_ge(z_setup_step, done[0])

            pool.wait_ge(w_rec_loaded, 16)
            then(pool.tensor_scalar(z_whole[:, :], w_rec_sb[:, P:2 * P], 0.5, None, ALU.mult))
            then(pool.tensor_copy(z_split[:, 0, :], z_whole[:, :]))
            then(pool.tensor_tensor(z_rest[:, :], z_whole[:, :], z_split[:, 0, :], ALU.subtract))
            then(pool.tensor_copy(z_split[:, 1, :], z_rest[:, :]))
            pool.tensor_tensor(z_split[:, 2, :], z_rest[:, :], z_split[:, 1, :], ALU.subtract).then_inc(w_z_ready, 1)

            def group(k, parity, at):
                if not has_a(at):
                    return
                route(k)

            def route(k):
                pool.wait_ge(neg_done, k)
                pool.tensor_tensor(exp_neg[:, :, :], euler[:, :, :], neg_logit[:, :, :], ALU.pow).then_inc(exp_done, 1)
                pool.wait_ge(exp_done, k)
                pool.tensor_tensor(one_plus[:, :, :], exp_neg[:, :, :], unit[:, :, :], ALU.add).then_inc(one_plus_done, 1)
                pool.wait_ge(score_done, k)
                rbias = small_sb[:, S_RBIAS:S_IOTA].rearrange("p (t e) -> p t e", e=E)
                pool.tensor_tensor(sel_score[:, :, :], score[:, :, :], rbias, ALU.add).then_inc(sel_done, 1)
                pool.wait_ge(picked_done, k)
                pool.tensor_tensor(mask[:, :, :], first[:, :, :], second[:, :, :], ALU.add).then_inc(mask_done, 1)
                pool.wait_ge(denom_done, k)
                pool.tensor_tensor(denom_eps[:, :], denom[:, :], epsilon[:, :], ALU.add).then_inc(denom_eps_done, 1)
                pool.wait_ge(scale_done, k)
                for out, data, scale in ((by_score, chosen, gate_scale), (by_half, mask, even_gate)):
                    pool.tensor_tensor(out[:, :, :], data[:, :, :],
                                       scale[:, :].rearrange("p (t e) -> p t e", e=1).broadcast_to([P, TILES, E]),
                                       ALU.mult).then_inc(gated_done, 1)
                pool.wait_ge(gated_done, k * 2)
                pool.tensor_tensor(combine[:, :, :], by_score[:, :, :], by_half[:, :, :], ALU.add).then_inc(combine_done, 1)
                pool.wait_ge(combine_done, k)

                def top(t):
                    return t[:, :, :].bitcast(BF16)[:, :, 1::2]

                pool.tensor_tensor(comb_rest[:, :, :], combine[:, :, :], top(combine), ALU.subtract).then_inc(comb_rest_done, 1)
                pool.tensor_copy(comb_parts[:, :, 0, :], top(combine))
                pool.wait_ge(comb_rest_done, k)
                pool.tensor_tensor(comb_parts[:, :, 2, :], comb_rest[:, :, :], top(comb_rest), ALU.subtract)
                pool.tensor_copy(comb_parts[:, :, 1, :], top(comb_rest)).then_inc(parts_done, 1)

            over_groups(pool, group)
            route(GROUPS)


def kernel(x, cond_1024, L0_cond_Wxz, L0_cond_bxz, L0_cond_Whz, L0_cond_bhz, L0_cond_Wxr, L0_cond_bxr, L0_cond_Whr,
           L0_cond_bhr, L0_cond_Wxh, L0_cond_bxh, L0_cond_Whh, L0_cond_bhh, L0_cond_Whq, L0_cond_bhq,
           L1_cond_router_w, L1_cond_router_t_w, L1_cond_router_bias, L1_cond_sw1, L1_cond_sw3, L1_cond_sw2,
           L1_cond_rw1, L1_cond_rw2):
    import ml_dtypes
    import numpy as np
    import concourse.bacc as _bacc
    from concourse.bass_utils import run_bass_kernel_spmd as _run

    def arr(a):
        return np.asarray(a)

    def side_by_side(*parts):
        return np.ascontiguousarray(np.concatenate(parts, axis=1))

    rw1 = arr(L1_cond_rw1).reshape(E * 64, C).T
    sw2 = arr(L1_cond_sw2).T.reshape(SHARED, P, C).transpose(1, 0, 2).reshape(P, SHARED * C)
    rw2 = arr(L1_cond_rw2).transpose(0, 2, 1).reshape(PAIRS, P, C).transpose(1, 0, 2).reshape(P, PAIRS * C)
    iota = np.tile(np.arange(E, dtype=np.float32), (P, TILES))
    chunk_of = np.arange(P) // 64
    select = np.zeros((3, E, PAIRS, P), ml_dtypes.bfloat16)
    for pair in range(PAIRS):
        for e in range(2):
            select[:, 2 * pair + e, pair, chunk_of == e] = 1
    arrays = {
        "x_t": np.ascontiguousarray(arr(x).transpose(2, 1, 0).reshape(C, T * B)),
        "w_in": side_by_side(arr(L0_cond_Wxr).T, arr(L0_cond_Wxz).T, arr(L0_cond_Wxh).T),
        "w_rec": side_by_side(arr(L0_cond_Whr).T, arr(L0_cond_Whz).T, arr(L0_cond_Whh).T),
        "w_moe": side_by_side(arr(L0_cond_Whq).T, arr(L1_cond_sw1).T, arr(L1_cond_sw3).T, rw1, sw2, rw2,
                              arr(L1_cond_router_w).T, arr(L1_cond_router_t_w).T),
        "small": side_by_side(np.tile(arr(cond_1024).T, (1, P // B)), arr(L0_cond_bhq)[:, None],
                              np.tile(arr(L1_cond_router_bias), (P, TILES)), iota,
                              np.stack([arr(L0_cond_bxr), arr(L0_cond_bxz), arr(L0_cond_bxh)], axis=1),
                              np.stack([arr(L0_cond_bhr), arr(L0_cond_bhz), arr(L0_cond_bhh)], axis=1)),
        "selectors": select.reshape(3 * E, PAIRS, P),
        "identity": np.eye(P, dtype=ml_dtypes.bfloat16),
        "gate_of_rows": np.repeat(np.tile(np.eye(3, dtype=ml_dtypes.bfloat16), (3, 1))[:, :, None], GT, axis=2),
    }
    nc = _bacc.Bacc("TRN2", target_bir_lowering=False, num_devices=1)
    args = [nc.dram_tensor(name, a.shape, mybir.dt.from_np(a.dtype), kind="ExternalInput").ap()
            for name, a in arrays.items()]
    out_t = nc.dram_tensor("out_t", (C, T * B), F32, kind="ExternalOutput").ap()
    gru_moe_program(nc, *args, out_t)
    result = _run(nc, [arrays], core_ids=[0])
    return np.ascontiguousarray(np.asarray(result.results[0]["out_t"]).reshape(C, T, B).transpose(2, 1, 0))
```

```python
from contextlib import ExitStack

import concourse.bass as bass
from concourse import mybir

F32 = mybir.dt.float32
BF16 = mybir.dt.bfloat16
F32R = mybir.dt.float32r
F16 = mybir.dt.float16
U32 = mybir.dt.uint32
ALU = mybir.AluOpType
ACT = mybir.ActivationFunctionType

P = 128
B, T, C, E = 32, 128, 128, 8
GS = 8
GT = GS * B
GROUPS = T // GS
TILES = GT // P
PAIR_BANK = (0, 1, 2, 2)
SHARED = 2
PAIRS = 4
PROJECT = ((5, 0), (6, 1), (7, 1))
READ_OUT, ROUTER, TURN_GATES = (0, 0), (1, 1), (7, 2)
SHARED_HIDDEN = ((2, 1), (2, 2), (3, 1), (3, 2))
ROUTED_HIDDEN = ((0, 1), (2, 0), (4, 0), (5, 1))
OUT_SHARED = ((1, 0), (1, 2))
OUT_ROUTED = ((3, 0), (4, 1), (6, 0), (7, 0))
WARM_UP = 17
IDLE_PRODUCTS = (3, 4)
BUSY_GAPS = (READ_OUT,) + SHARED_HIDDEN + PROJECT
HIDDEN_CUTS = 4
R_SEED_STEP, Z_SEED_STEP = 4, 5
EPS = 1e-9
EULER = 2.718281828459045

W_Q = 0
W_SW1 = W_Q + C
W_SW3 = W_SW1 + SHARED * P
W_RW1 = W_SW3 + SHARED * P
W_SW2 = W_RW1 + PAIRS * P
W_RW2 = W_SW2 + SHARED * C
W_ROUTER = W_RW2 + PAIRS * C
W_ROUTER_T = W_ROUTER + E
W_END = W_ROUTER_T + E
S_COND = 0
S_BHQ = S_COND + P
S_RBIAS = S_BHQ + 1
S_IOTA = S_RBIAS + TILES * E
S_BIAS_IN = S_IOTA + TILES * E
S_BIAS_REC = S_BIAS_IN + 3
S_END = S_BIAS_REC + 3
R_KEPT, R_UPD, H_RESET, RW_END = (P * i for i in range(4))


def gru_moe_program(nc: bass.Bass, x_t, w_in, w_rec, w_moe, small, selectors, identity, out_t):
    with ExitStack() as ctx:
        def sb(name, shape, dtype=F32):
            return ctx.enter_context(nc.sbuf_tensor(name, shape, dtype))

        def sem(name):
            return ctx.enter_context(nc.semaphore(name))

        def bank(name):
            return ctx.enter_context(nc.psum_tensor(name, [P, 512], F32))

        x_ring = sb("x_ring", [P, 2, GT])
        w_in_sb = sb("w_in_sb", [P, 3 * P])
        w_rec_sb = sb("w_rec_sb", [P, 3 * P])
        w_scaled = sb("w_scaled", [P, RW_END])
        z_whole = sb("z_whole", [P, P])
        z_rest = sb("z_rest", [P, P])
        z_split = sb("z_split", [P, 3, P], BF16)
        moe_w = sb("moe_w", [P, W_END])
        small_sb = sb("small_sb", [P, S_END])
        sel_sb = sb("sel_sb", [3 * E, PAIRS, P], BF16)
        ident = sb("ident", [P, P], BF16)
        bias_sum = sb("bias_sum", [P, 3])
        zeros = sb("zeros", [P, GT], BF16)
        table_out = sb("table_out", [P, 1])
        tanh_r = sb("tanh_r", [P, B])
        tanh_z = sb("tanh_z", [P, B])
        cand = sb("cand", [P, B])
        reset = sb("reset", [P, B])
        kept = sb("kept", [P, B])
        upd = sb("upd", [P, B])
        state_high = sb("state_high", [P, B], F16)
        state_low = sb("state_low", [P, B], F16)
        g_hist = sb("g_hist", [P, 2, GT])
        x1 = sb("x1", [P, 2, GT])
        x1_high = sb("x1_high", [P, 2, GT], F32R)
        x1_low = sb("x1_low", [P, 2, GT], F32R)
        hidden_high = sb("hidden_high", [P, W_SW2 - W_SW1], F32R)
        hidden_low = sb("hidden_low", [P, W_SW2 - W_SW1], F32R)
        silu_tanh = sb("silu_tanh", [P, SHARED, GT])
        silu_a = sb("silu_a", [P, SHARED, GT])
        hid_s = sb("hid_s", [P, 2, SHARED, GT])
        gelu = sb("gelu", [P, PAIRS, GT])
        hid_r = sb("hid_r", [P, PAIRS, GT])
        out_sb = sb("out_sb", [P, 2, GT])
        t_bias = sb("t_bias", [P, TILES, E])
        euler = sb("euler", [P, TILES, E])
        unit = sb("unit", [P, TILES, E])
        epsilon = sb("epsilon", [P, TILES])
        neg_logit = sb("neg_logit", [P, TILES, E])
        exp_neg = sb("exp_neg", [P, TILES, E])
        one_plus = sb("one_plus", [P, TILES, E])
        score = sb("score", [P, TILES, E])
        sel_score = sb("sel_score", [P, TILES, E])
        top8 = sb("top8", [P, TILES, 8])
        top8_at = sb("top8_at", [P, TILES, 8], U32)
        first = sb("first", [P, TILES, E])
        second = sb("second", [P, TILES, E])
        mask = sb("mask", [P, TILES, E])
        chosen = sb("chosen", [P, TILES, E])
        denom = sb("denom", [P, TILES])
        denom_eps = sb("denom_eps", [P, TILES])
        inverse = sb("inverse", [P, TILES])
        gate_scale = sb("gate_scale", [P, TILES])
        even_gate = sb("even_gate", [P, TILES])
        by_score = sb("by_score", [P, TILES, E])
        by_half = sb("by_half", [P, TILES, E])
        combine = sb("combine", [P, TILES, E])
        comb_rest = sb("comb_rest", [P, TILES, E])
        comb_parts = sb("comb_parts", [P, TILES, 3, E], BF16)
        comb_t = sb("comb_t", [3 * E, GT], BF16)

        bank_r, bank_z, bank_h = bank("bank_r"), bank("bank_z"), bank("bank_h")
        gate_bank = (bank_r, bank_z, bank_h)
        work = [bank("work0"), bank("work1"), bank("work2")]
        bank_o = bank("bank_o")
        bank_m = bank("bank_m")
        y_ps = bank_m[:, 0:GT]
        score_ps = bank_m[:, GT:GT + TILES * E]
        comb_ps = bank_o[0:3 * E, GT:GT + GT // 2].bitcast(BF16)
        late_comb_ps = bank_h[0:3 * E, GT:GT + GT // 2].bitcast(BF16)
        out_ps, late_out_ps = bank_o[:, 0:GT], bank_m[:, 0:GT]

        small_loaded, w_in_loaded, w_rec_loaded, moe_loaded = sem("small_loaded"), sem("w_in_loaded"), sem("w_rec_loaded"), sem("moe_loaded")
        x_loaded, out_free = [sem("x_loaded0"), sem("x_loaded1")], [sem("out_free0"), sem("out_free1")]
        setup_step, z_setup_step, zeroed, bank_opened, bias_ready = sem("setup_step"), sem("z_setup_step"), sem("zeroed"), sem("bank_opened"), sem("bias_ready")
        w_reset_ready, w_gates_ready, w_z_ready = sem("w_reset_ready"), sem("w_gates_ready"), sem("w_z_ready")
        g_init, tb_ps_done, moe_scaled = sem("g_init"), sem("tb_ps_done"), sem("moe_scaled")
        r_pre, z_pre, h_pre = sem("r_pre"), sem("z_pre"), sem("h_pre")
        r_ready, z_ready, cand_ready = sem("r_ready"), sem("z_ready"), sem("cand_ready")
        reset_ready, kept_ready, upd_ready = sem("reset_ready"), sem("kept_ready"), sem("upd_ready")
        state_split = sem("state_split")
        half_seeded = sem("half_seeded")
        g_done = sem("g_done")
        y_done, scores_done, comb_t_done = sem("y_done"), sem("scores_done"), sem("comb_t_done")
        silu_pre, gelu_pre, out_done = sem("silu_pre"), sem("gelu_pre"), sem("out_done")
        silu_tanh_done, gelu_done, comb_copied = sem("silu_tanh_done"), sem("gelu_done"), sem("comb_copied")
        x1_high_done, x1_low_done = sem("x1_high_done"), sem("x1_low_done")
        hidden_high_done, hidden_split = sem("hidden_high_done"), sem("hidden_split")
        x1_done, silu_a_done, hid_s_done, hid_r_done = sem("x1_done"), sem("silu_a_done"), sem("hid_s_done"), sem("hid_r_done")
        final_done, late_gates_done = sem("final_done"), sem("late_gates_done")
        neg_done, score_done, top_done, top_at_done = sem("neg_done"), sem("score_done"), sem("top_done"), sem("top_at_done")
        picked_done, denom_done, inverse_done, scale_done = sem("picked_done"), sem("denom_done"), sem("inverse_done"), sem("scale_done")
        exp_done, one_plus_done, sel_done = sem("exp_done"), sem("one_plus_done"), sem("sel_done")
        constants_set, mask_done, denom_eps_done = sem("constants_set"), sem("mask_done"), sem("denom_eps_done")
        gated_done, combine_done, comb_rest_done, parts_done = sem("gated_done"), sem("combine_done"), sem("comb_rest_done"), sem("parts_done")

        def over_groups(eng, group):
            group(0, 0, 0)
            group(1, 1, 1)
            with eng.Fori(0, (GROUPS - 4) // 4) as quad:
                for n in range(4):
                    group(quad * 4 + (2 + n), n % 2, None)
            group(GROUPS - 2, 0, GROUPS - 2)
            group(GROUPS - 1, 1, GROUPS - 1)

        def has_next(at):
            return at is None or at < GROUPS - 1

        def has_a(at):
            return at is None or at >= 1

        def has_b(at):
            return at is None or at >= 2

        def hidden_cut(n):
            width = (W_SW2 - W_SW1) // HIDDEN_CUTS
            return n * width, (n + 1) * width

        def weighted(data, scale):
            return data[:, :, :], scale[:, :].rearrange("p (t e) -> p t e", e=1).broadcast_to([P, TILES, E])

        def gate_parts(eng, k):
            eng.wait_ge(scale_done, k)
            eng.tensor_tensor(by_score[:, :, :], *weighted(chosen, gate_scale), ALU.mult)
            eng.tensor_tensor(by_half[:, :, :], *weighted(mask, even_gate), ALU.mult).then_inc(gated_done, 1)
            eng.wait_ge(gated_done, k)
            eng.tensor_tensor(combine[:, :, :], by_score[:, :, :], by_half[:, :, :], ALU.add).then_inc(combine_done, 1)
            eng.wait_ge(combine_done, k)

            def top(t):
                return t[:, :, :].bitcast(BF16)[:, :, 1::2]

            eng.tensor_tensor(comb_rest[:, :, :], combine[:, :, :], top(combine), ALU.subtract).then_inc(comb_rest_done, 1)
            eng.tensor_copy(comb_parts[:, :, 0, :], top(combine))
            eng.wait_ge(comb_rest_done, k)
            eng.tensor_tensor(comb_parts[:, :, 2, :], comb_rest[:, :, :], top(comb_rest), ALU.subtract)
            eng.tensor_copy(comb_parts[:, :, 1, :], top(comb_rest)).then_inc(parts_done, 1)

        def tail_bank(pair):
            return bank_h if pair == 3 else work[PAIR_BANK[pair]]

        def late_hidden(pair):
            return (bank_r, bank_z)[pair // 2][:, pair % 2 * GT:(pair % 2 + 1) * GT]

        def late_gate(pair):
            return (work[0], work[1], work[2], bank_h)[pair][:, 0:GT]

        block = ctx.enter_context(nc.Block())

        @block.sync
        def _(sp):
            for half in out_free:
                sp.sem_inc(half, 16)
            sp.dma_start(x_ring[:, 0, :], x_t[:, 0:GT]).then_inc(x_loaded[0], 16)
            sp.dma_start(w_in_sb[:, :], w_in).then_inc(w_in_loaded, 16)
            sp.dma_start(x_ring[:, 1, :], x_t[:, GT:2 * GT]).then_inc(x_loaded[1], 16)
            sp.dma_start(moe_w[:, :], w_moe).then_inc(moe_loaded, 16)
            sp.dma_start(sel_sb[:, :, :], selectors).then_inc(moe_loaded, 16)

            def store(k, parity):
                sp.wait_ge(final_done, k - 1)
                sp.dma_start(out_t[:, bass.ds((k - 2) * GT, GT)], out_sb[:, parity, :]).then_inc(out_free[parity], 16)

            def group(k, parity, at):
                if has_a(at) and has_next(at):
                    sp.wait_ge(x1_done, k)
                    sp.dma_start(x_ring[:, 1 - parity, :],
                                 x_t[:, bass.ds((k + 1) * GT, GT)]).then_inc(x_loaded[1 - parity], 16)
                if has_b(at):
                    store(k, parity)

            over_groups(sp, group)
            store(GROUPS, 0)
            store(GROUPS + 1, 1)
            for half in out_free:
                sp.wait_ge(half, 16 + 16 * GROUPS // 2)

        @block.tensor
        def _(pe):
            def recur(dst, col, weights, data):
                return pe.matmul(dst[:, col:col + B], w_scaled[:, weights:weights + P], data[:, :],
                                 start=False, stop=True, skip_group_check=True)

            def recur_z(col, data, part):
                for m in range(3 - part):
                    last = pe.matmul(bank_z[:, col:col + B], z_split[:, m, :], data[:, :],
                                     start=False, stop=True, skip_group_check=True)
                return last

            def project(gate, parity):
                pe.matmul(gate_bank[gate][:, parity * GT:(parity + 1) * GT], w_in_sb[:, gate * P:(gate + 1) * P],
                          x_ring[:, parity, :], start=False, stop=True, skip_group_check=True)

            def keep_warm(n, dst=bank_o[:, 0:GT], start=True):
                for _ in range(n):
                    pe.matmul(dst, zeros[:, 0:P], zeros[:, :], start=start, stop=True, skip_group_check=True)

            def weights(col, width=P):
                return moe_w[:, col:col + width]

            def hidden(dst, col, half):
                col -= W_SW1
                for n, (w, x) in enumerate(((hidden_high, x1_high), (hidden_low, x1_high), (hidden_high, x1_low))):
                    last = pe.matmul(dst, w[:, col:col + P], x[:, half, :], start=(n == 0), stop=(n == 2))
                return last

            def read_out(k, a):
                pe.wait_ge(g_done, k * GS)
                pe.matmul(y_ps, weights(W_Q), g_hist[:, a, :], start=True, stop=True).then_inc(y_done, 1)

            def router(k, a, tile):
                if tile == 0:
                    pe.wait_ge(x1_done, k)
                mm = pe.matmul(score_ps[:, tile * E:(tile + 1) * E], x1[:, a, tile * P:(tile + 1) * P],
                               weights(W_ROUTER, E), start=True, stop=True)
                if tile == TILES - 1:
                    mm.then_inc(scores_done, 1)

            def shared_hidden(k, a, chunk, with_b, half):
                dst = work[chunk]
                if half == 0:
                    if chunk == 0:
                        pe.wait_ge(x1_low_done, k)
                    if with_b:
                        pe.wait_ge(hid_r_done, (k - 2) * PAIRS + chunk + 1)
                    hidden(dst[:, 0:GT], W_SW1 + chunk * P, a)
                else:
                    hidden(dst[:, GT:2 * GT], W_SW3 + chunk * P, a).then_inc(silu_pre, 1)

            def routed_hidden(k, b, pair, dst=None):
                if pair == 0:
                    pe.wait_ge(comb_copied, k - 1)
                    pe.wait_ge(hid_s_done, (k - 2) * SHARED + 1)
                elif pair == 1:
                    pe.wait_ge(hid_s_done, (k - 1) * SHARED)
                elif pair == 3 and dst is None:
                    pe.wait_ge(hid_r_done, (k - 2) * PAIRS + 3)
                dst = dst or work[PAIR_BANK[pair]]
                pe.matmul(dst[:, GT:2 * GT], sel_sb[:, pair, :], comb_t[:, :], start=True, stop=True)
                hidden(dst[:, 0:GT], W_RW1 + pair * P, b).then_inc(gelu_pre, 1)

            def out_shared(k, b, chunk, dst=out_ps):
                pe.matmul(dst, weights(W_SW2 + chunk * C), hid_s[:, b, chunk, :],
                          start=(chunk == 0), stop=False)

            def out_routed(k, pair, dst=out_ps):
                pe.wait_ge(hid_r_done, (k - 2) * PAIRS + pair + 1)
                mm = pe.matmul(dst, weights(W_RW2 + pair * C), hid_r[:, pair, :],
                               start=False, stop=(pair == PAIRS - 1))
                if pair == PAIRS - 1:
                    mm.then_inc(out_done, 1)

            def turn_gates(k, dst):
                pe.wait_ge(parts_done, k)
                for tile in range(TILES):
                    mm = pe.transpose(dst[:, tile * P:(tile + 1) * P],
                                      comb_parts[:, tile, :, :].rearrange("p m e -> p (m e)"), ident[:, :])
                mm.then_inc(comb_t_done, 1)

            pe.wait_ge(zeroed, 1)
            for dst in gate_bank:
                keep_warm(1, dst[:, 0:GT])
                pe.matmul(dst[:, GT:2 * GT], zeros[:, 0:P], zeros[:, :],
                          start=False, stop=True, skip_group_check=True).then_inc(bank_opened, 1)
            keep_warm(WARM_UP)
            pe.wait_ge(x_loaded[0], 16)
            pe.wait_ge(w_in_loaded, 16)
            pe.wait_ge(w_rec_loaded, 16)
            cond = small_sb[:, S_COND:S_COND + B]
            pe.wait_ge(half_seeded, 1)
            project(0, 0)
            pe.matmul(bank_r[:, 0:B], w_rec_sb[:, 0:P], cond,
                      start=False, stop=True, skip_group_check=True).then_inc(r_pre, 1)
            pe.wait_ge(half_seeded, 2)
            project(1, 0)
            pe.matmul(bank_z[:, 0:B], w_rec_sb[:, P:2 * P], cond,
                      start=False, stop=True, skip_group_check=True).then_inc(z_pre, 1)
            pe.wait_ge(half_seeded, 3)
            project(2, 0)
            pe.wait_ge(w_reset_ready, 1)

            def group(k, parity, at):
                a, b = 1 - parity, parity

                def fill(slot):
                    if has_next(at):
                        if slot == PROJECT[0]:
                            pe.wait_ge(x_loaded[1 - parity], x_count(k, parity))
                        if slot in PROJECT:
                            gate = PROJECT.index(slot)
                            pe.wait_ge(half_seeded, (k + 1) * 3 + gate + 1)
                            project(gate, 1 - parity)
                    elif slot in PROJECT:
                        if slot == PROJECT[2]:
                            pe.wait_ge(cand_ready, k * GS + GS)
                        keep_warm(4, gate_bank[PROJECT.index(slot)][:, 0:GT], start=False)
                    if has_a(at):
                        if slot == READ_OUT:
                            read_out(k, a)
                        if slot == ROUTER:
                            router(k, a, 0)
                            router(k, a, 1)
                        if slot in SHARED_HIDDEN:
                            n = SHARED_HIDDEN.index(slot)
                            shared_hidden(k, a, n // 2, has_b(at), n % 2)
                    if has_b(at):
                        if slot in OUT_SHARED:
                            out_shared(k, b, OUT_SHARED.index(slot))
                        if slot in OUT_ROUTED:
                            out_routed(k, OUT_ROUTED.index(slot))
                        if slot in ROUTED_HIDDEN:
                            routed_hidden(k, b, ROUTED_HIDDEN.index(slot))
                    elif slot[1] < 2 and slot not in (BUSY_GAPS if has_a(at) else PROJECT):
                        keep_warm(IDLE_PRODUCTS[slot[1]])
                    if not has_next(at) and slot == TURN_GATES:
                        read_out(GROUPS, parity)
                    if has_a(at) and slot == TURN_GATES:
                        if has_b(at):
                            pe.wait_ge(final_done, k - 1)
                        turn_gates(k, comb_ps)

                if at == 1:
                    pe.wait_ge(hidden_split, HIDDEN_CUTS)

                for s in range(GS):
                    here = parity * GT + s * B
                    nxt = here + B if s < GS - 1 else (1 - parity) * GT
                    pe.wait_ge(reset_ready, k * GS + s + 1)
                    recur(bank_h, here, H_RESET, reset).then_inc(h_pre, 1)
                    if at == 0 and s == 0:
                        pe.wait_ge(w_gates_ready, 1)
                    if at == 0 and s == GS // 2:
                        pe.wait_ge(moe_scaled, 1)
                        pe.matmul(score_ps[:, 0:E], small_sb[:, S_COND:S_COND + P], weights(W_ROUTER_T, E),
                                  start=True, stop=True).then_inc(tb_ps_done, 1)
                    fill((s, 0))
                    if has_next(at) or s < GS - 1:
                        pe.wait_ge(kept_ready, k * GS + s + 1)
                        recur(bank_r, nxt, R_KEPT, kept)
                        pe.wait_ge(upd_ready, k * GS + s + 1)
                        recur(bank_r, nxt, R_UPD, upd).then_inc(r_pre, 1)
                    fill((s, 1))
                    if has_next(at) or s < GS - 1:
                        if at == 0 and s == 0:
                            pe.wait_ge(w_z_ready, 1)
                        if has_next(at) and s == Z_SEED_STEP:
                            pe.wait_ge(half_seeded, (k + 1) * 3 + 2)
                        for part, data in enumerate((state_high, state_low)):
                            pe.wait_ge(state_split, (k * GS + s) * 2 + part + 1)
                            mm = recur_z(nxt, data, part)
                        mm.then_inc(z_pre, 1)
                    fill((s, 2))

            def x_count(k, parity):
                return (k + 1 - (1 - parity)) * 8 + 16

            over_groups(pe, group)

            k, a, b = GROUPS, 1, 0
            routed_hidden(k, b, 0)
            router(k, a, 0)
            router(k, a, 1)
            routed_hidden(k, b, 1)
            pe.wait_ge(final_done, k - 2)
            out_shared(k, b, 0)
            routed_hidden(k, b, 2)
            out_shared(k, b, 1)
            routed_hidden(k, b, 3, tail_bank(3))
            for chunk in range(SHARED):
                shared_hidden(k, a, chunk, True, 0)
                shared_hidden(k, a, chunk, True, 1)
            for pair in range(PAIRS):
                out_routed(k, pair)
                mm = hidden(late_hidden(pair), W_RW1 + pair * P, a)
                if pair % 2:
                    mm.then_inc(gelu_pre, 2)
            pe.wait_ge(hid_s_done, k * SHARED)
            out_shared(k + 1, a, 0, late_out_ps)
            out_shared(k + 1, a, 1, late_out_ps)
            turn_gates(k, late_comb_ps)
            pe.wait_ge(comb_copied, k)
            for pair in range(PAIRS):
                pe.matmul(late_gate(pair), sel_sb[:, pair, :], comb_t[:, :], start=True, stop=True).then_inc(late_gates_done, 1)
            for pair in range(PAIRS):
                out_routed(k + 1, pair, late_out_ps)

        @block.scalar
        def _(act):
            act.dma_start(small_sb[:, :], small).then_inc(small_loaded, 16)
            act.dma_start(ident[:, :], identity).then_inc(small_loaded, 16)
            act.dma_start(w_rec_sb[:, :], w_rec).then_inc(w_rec_loaded, 16)
            act.wait_ge(zeroed, 1)
            act.activation(table_out[:, :], zeros[:, 0:1], ACT.Gelu)

            def seed_half(gate, parity):
                act.activation(gate_bank[gate][:, parity * GT:(parity + 1) * GT], zeros[:, :], ACT.Identity,
                               bias=bias_sum[:, gate:gate + 1]).then_inc(half_seeded, 1)

            act.wait_ge(bias_ready, 1)
            for gate in range(3):
                act.wait_ge(bank_opened, gate + 1)
                seed_half(gate, 0)

            def silu_gate(k, chunk):
                act.wait_ge(silu_pre, (k - 1) * SHARED + chunk + 1)
                act.activation(silu_tanh[:, chunk, :], work[chunk][:, 0:GT], ACT.Tanh, scale=0.5).then_inc(silu_tanh_done, 1)

            def gelu_of(k, pair, src):
                act.wait_ge(gelu_pre, (k - 2) * PAIRS + pair + 1)
                act.activation(gelu[:, pair, :], src, ACT.Gelu).then_inc(gelu_done, 1)

            def keep_gates(k, src):
                act.wait_ge(comb_t_done, k - 1)
                act.activation(comb_t[:, :], src, ACT.Copy).then_inc(comb_copied, 1)

            def round_x1(k, a):
                act.wait_ge(x1_done, k)
                act.activation(x1_high[:, a, :], x1[:, a, :], ACT.Copy).then_inc(x1_high_done, 1)

            def group(k, parity, at):
                for s in range(GS):
                    col = parity * GT + s * B
                    act.wait_ge(r_pre, k * GS + s + 1)
                    act.activation(tanh_r[:, :], bank_r[:, col:col + B], ACT.Tanh, scale=0.5).then_inc(r_ready, 1)
                    if has_next(at) and s == R_SEED_STEP:
                        seed_half(0, 1 - parity)
                    act.wait_ge(z_pre, k * GS + s + 1)
                    act.activation(tanh_z[:, :], bank_z[:, col:col + B], ACT.Tanh, scale=0.5).then_inc(z_ready, 1)
                    act.wait_ge(h_pre, k * GS + s + 1)
                    act.activation(cand[:, :], bank_h[:, col:col + B], ACT.Tanh).then_inc(cand_ready, 1)
                    if has_b(at) and s == 0:
                        keep_gates(k, comb_ps)
                    if has_next(at) and s in (Z_SEED_STEP, GS - 1):
                        seed_half(1 if s == Z_SEED_STEP else 2, 1 - parity)
                    if has_a(at) and s in (3, 4):
                        silu_gate(k, s - 3)
                    if has_a(at) and s == 1:
                        round_x1(k, 1 - parity)
                    if at == 0 and 3 <= s < 3 + HIDDEN_CUTS:
                        if s == 3:
                            act.wait_ge(moe_loaded, 32)
                        lo, hi = hidden_cut(s - 3)
                        act.activation(hidden_high[:, lo:hi], moe_w[:, W_SW1 + lo:W_SW1 + hi], ACT.Copy).then_inc(hidden_high_done, 1)
                    if has_b(at) and s in (1, 2, 4, 6):
                        pair = (1, 2, 4, 6).index(s)
                        gelu_of(k, pair, work[PAIR_BANK[pair]][:, 0:GT])

            over_groups(act, group)

            k = GROUPS
            keep_gates(k, comb_ps)
            round_x1(k, 1)
            for pair in range(PAIRS):
                gelu_of(k, pair, tail_bank(pair)[:, 0:GT])
            for chunk in range(SHARED):
                silu_gate(k, chunk)
            for pair in range(PAIRS):
                gelu_of(k + 1, pair, late_hidden(pair))
            keep_gates(k + 1, late_comb_ps)

        @block.vector
        def _(dve):
            done = [0]

            def then(ins):
                done[0] += 1
                ins.then_inc(setup_step, 1)
                dve.wait_ge(setup_step, done[0])

            dve.memset(zeros[:, :], 0.0).then_inc(zeroed, 1)
            dve.wait_ge(small_loaded, 32)
            dve.tensor_tensor(bias_sum[:, :], small_sb[:, S_BIAS_IN:S_BIAS_REC], small_sb[:, S_BIAS_REC:S_END],
                              ALU.add).then_inc(bias_ready, 1)
            dve.tensor_scalar(g_hist[:, 1, GT - B:GT], small_sb[:, S_COND:S_COND + B], 2.0, None, ALU.mult).then_inc(g_init, 1)

            def scale_weights(dst, gate, factor):
                return dve.tensor_scalar(w_scaled[:, dst:dst + P], w_rec_sb[:, gate * P:(gate + 1) * P], factor, None, ALU.mult)

            dve.wait_ge(w_rec_loaded, 16)
            scale_weights(H_RESET, 2, 0.25).then_inc(w_reset_ready, 1)
            scale_weights(R_KEPT, 0, 0.25)
            scale_weights(R_UPD, 0, -0.5).then_inc(w_gates_ready, 1)

            def experts_setup():
                dve.wait_ge(moe_loaded, 32)
                then(dve.tensor_scalar(moe_w[:, W_Q:W_Q + C], moe_w[:, W_Q:W_Q + C], 0.5, None, ALU.mult))
                dve.tensor_scalar(moe_w[:, W_SW2:W_RW2], moe_w[:, W_SW2:W_RW2], 0.5, None, ALU.mult).then_inc(moe_scaled, 1)

            def keep_cond_scores():
                dve.wait_ge(tb_ps_done, 1)
                for tile in range(TILES):
                    ins = dve.tensor_copy(t_bias[:, tile, :], score_ps[:, 0:E])
                then(ins)

            def residual(k, a):
                dve.wait_ge(y_done, k)
                dve.scalar_tensor_tensor(out=x1[:, a, :], in0=y_ps, scalar=small_sb[:, S_BHQ:S_BHQ + 1],
                                         in1=x_ring[:, a, :], op0=ALU.add, op1=ALU.add).then_inc(x1_done, 1)

            def rest_of_x1(k, a):
                dve.wait_ge(x1_high_done, k)
                dve.tensor_tensor(x1_low[:, a, :], x1[:, a, :], x1_high[:, a, :].bitcast(F32), ALU.subtract).then_inc(x1_low_done, 1)

            def negate_logits(k):
                dve.wait_ge(scores_done, k)
                dve.scalar_tensor_tensor(out=neg_logit[:, :, :], in0=score_ps.rearrange("p (t e) -> p t e", e=E), scalar=-1.0,
                                         in1=t_bias[:, :, :], op0=ALU.mult, op1=ALU.subtract).then_inc(neg_done, 1)

            def sigmoid_scores(k):
                dve.wait_ge(one_plus_done, k)
                dve.reciprocal(score[:, :, :], one_plus[:, :, :]).then_inc(score_done, 1)

            def sort_scores():
                for tile in range(TILES):
                    ins = dve.max(top8[:, tile, :], sel_score[:, tile, :])
                ins.then_inc(top_done, 1)

            def sorted_experts():
                for tile in range(TILES):
                    ins = dve.max_index(top8_at[:, tile, :], top8[:, tile, :], sel_score[:, tile, :])
                ins.then_inc(top_at_done, 1)

            def pick_two(k):
                dve.wait_ge(top_at_done, k)
                iota = small_sb[:, S_IOTA:S_BIAS_IN].rearrange("p (t e) -> p t e", e=E)
                for n, pick in enumerate((first, second)):
                    ins = dve.tensor_tensor(pick[:, :, :], iota, top8_at[:, :, n:n + 1].broadcast_to([P, TILES, E]), ALU.is_equal)
                ins.then_inc(picked_done, 1)

            def sum_chosen(k):
                dve.wait_ge(mask_done, k)
                for tile in range(TILES):
                    ins = dve.tensor_tensor_reduce(chosen[:, tile, :], mask[:, tile, :], score[:, tile, :], 1.0, 0.0,
                                                   ALU.mult, ALU.add, denom[:, tile:tile + 1])
                ins.then_inc(denom_done, 1)

            def invert_sum(k):
                dve.wait_ge(denom_eps_done, k)
                dve.reciprocal(inverse[:, :], denom_eps[:, :]).then_inc(inverse_done, 1)
                dve.tensor_scalar(even_gate[:, :], denom[:, :], EPS, 0.5, ALU.is_le, ALU.mult)

            def scale_gates(k):
                dve.wait_ge(inverse_done, k)
                dve.scalar_tensor_tensor(out=gate_scale[:, :], in0=denom[:, :], scalar=EPS,
                                         in1=inverse[:, :], op0=ALU.is_gt, op1=ALU.mult).then_inc(scale_done, 1)

            def silu_first(k, chunk):
                dve.wait_ge(silu_tanh_done, (k - 1) * SHARED + chunk + 1)
                dve.scalar_tensor_tensor(out=silu_a[:, chunk, :], in0=silu_tanh[:, chunk, :], scalar=1.0,
                                         in1=work[chunk][:, 0:GT], op0=ALU.add, op1=ALU.mult).then_inc(silu_a_done, 1)

            def silu_second(k, a, chunk):
                dve.wait_ge(silu_a_done, (k - 1) * SHARED + chunk + 1)
                dve.tensor_tensor(hid_s[:, a, chunk, :], silu_a[:, chunk, :],
                                  work[chunk][:, GT:2 * GT], ALU.mult).then_inc(hid_s_done, 1)

            def gate_hidden(k, pair, gate):
                dve.wait_ge(gelu_done, (k - 2) * PAIRS + pair + 1)
                dve.tensor_tensor(hid_r[:, pair, :], gelu[:, pair, :], gate, ALU.mult).then_inc(hid_r_done, 1)

            def finish(k, b, src=out_ps):
                dve.wait_ge(out_done, k - 1)
                dve.wait_ge(out_free[b], (k - b) * 8)
                dve.scalar_tensor_tensor(out=out_sb[:, b, :], in0=src, scalar=1.0 / 3.0,
                                         in1=x1[:, b, :], op0=ALU.mult, op1=ALU.add).then_inc(final_done, 1)

            def group(k, parity, at):
                a, b = 1 - parity, parity

                def fill(slot):
                    if has_b(at) and slot == (0, 0):
                        silu_second(k - 1, b, 1)
                    if has_a(at):
                        if slot == (1, 0):
                            residual(k, a)
                        if slot == (1, 2):
                            rest_of_x1(k, a)
                        if slot == (3, 2):
                            sigmoid_scores(k)
                        if slot == (2, 0):
                            negate_logits(k)
                        if slot == (4, 0):
                            silu_first(k, 0)
                            dve.wait_ge(sel_done, k)
                        if slot == (4, 2):
                            sort_scores()
                        if slot == (5, 0):
                            dve.wait_ge(top_done, k)
                        if slot == (5, 1):
                            sorted_experts()
                        if slot == (5, 2):
                            pick_two(k)
                        if slot == (6, 0):
                            silu_first(k, 1)
                        if slot == (6, 1):
                            sum_chosen(k)
                        if slot == (7, 0):
                            invert_sum(k)
                            scale_gates(k)
                            silu_second(k, a, 0)
                    pair = {(2, 0): 0, (3, 0): 1, (5, 0): 2, (6, 2): 3}.get(slot)
                    if has_b(at) and pair is not None:
                        gate_hidden(k, pair, work[PAIR_BANK[pair]][:, GT:2 * GT])
                    if has_b(at) and slot == (7, 2):
                        finish(k, b)

                for s in range(GS):
                    t = k * GS + s
                    before = g_hist[:, parity, (s - 1) * B:s * B] if s else g_hist[:, 1 - parity, GT - B:GT]
                    if at == 0 and s == 0:
                        dve.wait_ge(g_init, 1)
                    dve.wait_ge(r_ready, t + 1)
                    dve.scalar_tensor_tensor(out=reset[:, :], in0=tanh_r[:, :], scalar=1.0, in1=before,
                                             op0=ALU.add, op1=ALU.mult).then_inc(reset_ready, 1)
                    fill((s, 0))
                    dve.wait_ge(z_ready, t + 1)
                    dve.scalar_tensor_tensor(out=kept[:, :], in0=tanh_z[:, :], scalar=1.0, in1=before,
                                             op0=ALU.add, op1=ALU.mult).then_inc(kept_ready, 1)
                    fill((s, 1))
                    dve.wait_ge(cand_ready, t + 1)
                    dve.scalar_tensor_tensor(out=upd[:, :], in0=tanh_z[:, :], scalar=1.0, in1=cand[:, :],
                                             op0=ALU.subtract, op1=ALU.mult).then_inc(upd_ready, 1)
                    state = g_hist[:, parity, s * B:(s + 1) * B]
                    dve.wait_ge(upd_ready, t + 1)
                    dve.scalar_tensor_tensor(out=state, in0=kept[:, :], scalar=0.5,
                                             in1=upd[:, :], op0=ALU.mult, op1=ALU.subtract).then_inc(g_done, 1)
                    dve.scalar_tensor_tensor(out=state_high[:, :], in0=kept[:, :], scalar=0.5,
                                             in1=upd[:, :], op0=ALU.mult, op1=ALU.subtract).then_inc(state_split, 1)
                    dve.wait_ge(state_split, t * 2 + 1)
                    dve.tensor_tensor(state_low[:, :], state, state_high[:, :], ALU.subtract).then_inc(state_split, 1)
                    if at == 0 and 4 <= s < 4 + HIDDEN_CUTS:
                        dve.wait_ge(hidden_high_done, s - 3)
                        lo, hi = hidden_cut(s - 4)
                        dve.tensor_tensor(hidden_low[:, lo:hi], moe_w[:, W_SW1 + lo:W_SW1 + hi],
                                          hidden_high[:, lo:hi].bitcast(F32), ALU.subtract).then_inc(hidden_split, 1)
                    if at == 0 and s == GS // 4:
                        experts_setup()
                    if at == 0 and s == GS - 2:
                        keep_cond_scores()
                    fill((s, 2))

            over_groups(dve, group)

            k, a, b = GROUPS, 1, 0
            dve.wait_ge(final_done, k - 2)
            residual(k, a)
            silu_second(k - 1, b, 1)
            rest_of_x1(k, a)
            negate_logits(k)
            for pair in range(PAIRS):
                gate_hidden(k, pair, tail_bank(pair)[:, GT:2 * GT])
            sigmoid_scores(k)
            silu_first(k, 0)
            dve.wait_ge(sel_done, k)
            sort_scores()
            dve.wait_ge(top_done, k)
            sorted_experts()
            silu_first(k, 1)
            pick_two(k)
            silu_second(k, a, 0)
            sum_chosen(k)
            silu_second(k, a, 1)
            invert_sum(k)
            scale_gates(k)
            gate_parts(dve, k)
            finish(k, b)
            for pair in range(PAIRS):
                dve.wait_ge(late_gates_done, pair + 1)
                gate_hidden(k + 1, pair, late_gate(pair))
            finish(k + 1, a, late_out_ps)

        @block.gpsimd
        def _(pool):
            pool.memset(euler[:, :, :], EULER)
            pool.memset(unit[:, :, :], 1.0)
            pool.memset(epsilon[:, :], EPS).then_inc(constants_set, 1)
            pool.wait_ge(constants_set, 1)
            done = [0]

            def then(ins):
                done[0] += 1
                ins.then_inc(z_setup_step, 1)
                pool.wait_ge(z_setup_step, done[0])

            pool.wait_ge(w_rec_loaded, 16)
            then(pool.tensor_scalar(z_whole[:, :], w_rec_sb[:, P:2 * P], 0.5, None, ALU.mult))
            then(pool.tensor_copy(z_split[:, 0, :], z_whole[:, :]))
            then(pool.tensor_tensor(z_rest[:, :], z_whole[:, :], z_split[:, 0, :], ALU.subtract))
            then(pool.tensor_copy(z_split[:, 1, :], z_rest[:, :]))
            pool.tensor_tensor(z_split[:, 2, :], z_rest[:, :], z_split[:, 1, :], ALU.subtract).then_inc(w_z_ready, 1)

            def group(k, parity, at):
                if not has_a(at):
                    return
                route(k)
                gate_parts(pool, k)

            def route(k):
                pool.wait_ge(neg_done, k)
                pool.tensor_tensor(exp_neg[:, :, :], euler[:, :, :], neg_logit[:, :, :], ALU.pow).then_inc(exp_done, 1)
                pool.wait_ge(exp_done, k)
                pool.tensor_tensor(one_plus[:, :, :], exp_neg[:, :, :], unit[:, :, :], ALU.add).then_inc(one_plus_done, 1)
                pool.wait_ge(score_done, k)
                rbias = small_sb[:, S_RBIAS:S_IOTA].rearrange("p (t e) -> p t e", e=E)
                pool.tensor_tensor(sel_score[:, :, :], score[:, :, :], rbias, ALU.add).then_inc(sel_done, 1)
                pool.wait_ge(picked_done, k)
                pool.tensor_tensor(mask[:, :, :], first[:, :, :], second[:, :, :], ALU.add).then_inc(mask_done, 1)
                pool.wait_ge(denom_done, k)
                pool.tensor_tensor(denom_eps[:, :], denom[:, :], epsilon[:, :], ALU.add).then_inc(denom_eps_done, 1)

            over_groups(pool, group)
            route(GROUPS)


def kernel(x, cond_1024, L0_cond_Wxz, L0_cond_bxz, L0_cond_Whz, L0_cond_bhz, L0_cond_Wxr, L0_cond_bxr, L0_cond_Whr,
           L0_cond_bhr, L0_cond_Wxh, L0_cond_bxh, L0_cond_Whh, L0_cond_bhh, L0_cond_Whq, L0_cond_bhq,
           L1_cond_router_w, L1_cond_router_t_w, L1_cond_router_bias, L1_cond_sw1, L1_cond_sw3, L1_cond_sw2,
           L1_cond_rw1, L1_cond_rw2):
    import ml_dtypes
    import numpy as np
    import concourse.bacc as _bacc
    from concourse.bass_utils import run_bass_kernel_spmd as _run

    def arr(a):
        return np.asarray(a)

    def side_by_side(*parts):
        return np.ascontiguousarray(np.concatenate(parts, axis=1))

    rw1 = arr(L1_cond_rw1).reshape(E * 64, C).T
    sw2 = arr(L1_cond_sw2).T.reshape(SHARED, P, C).transpose(1, 0, 2).reshape(P, SHARED * C)
    rw2 = arr(L1_cond_rw2).transpose(0, 2, 1).reshape(PAIRS, P, C).transpose(1, 0, 2).reshape(P, PAIRS * C)
    iota = np.tile(np.arange(E, dtype=np.float32), (P, TILES))
    chunk_of = np.arange(P) // 64
    select = np.zeros((3, E, PAIRS, P), ml_dtypes.bfloat16)
    for pair in range(PAIRS):
        for e in range(2):
            select[:, 2 * pair + e, pair, chunk_of == e] = 1
    arrays = {
        "x_t": np.ascontiguousarray(arr(x).transpose(2, 1, 0).reshape(C, T * B)),
        "w_in": side_by_side(arr(L0_cond_Wxr).T, arr(L0_cond_Wxz).T, arr(L0_cond_Wxh).T),
        "w_rec": side_by_side(arr(L0_cond_Whr).T, arr(L0_cond_Whz).T, arr(L0_cond_Whh).T),
        "w_moe": side_by_side(arr(L0_cond_Whq).T, arr(L1_cond_sw1).T, arr(L1_cond_sw3).T, rw1, sw2, rw2,
                              arr(L1_cond_router_w).T, arr(L1_cond_router_t_w).T),
        "small": side_by_side(np.tile(arr(cond_1024).T, (1, P // B)), arr(L0_cond_bhq)[:, None],
                              np.tile(arr(L1_cond_router_bias), (P, TILES)), iota,
                              np.stack([arr(L0_cond_bxr), arr(L0_cond_bxz), arr(L0_cond_bxh)], axis=1),
                              np.stack([arr(L0_cond_bhr), arr(L0_cond_bhz), arr(L0_cond_bhh)], axis=1)),
        "selectors": select.reshape(3 * E, PAIRS, P),
        "identity": np.eye(P, dtype=ml_dtypes.bfloat16),
    }
    nc = _bacc.Bacc("TRN2", target_bir_lowering=False, num_devices=1)
    args = [nc.dram_tensor(name, a.shape, mybir.dt.from_np(a.dtype), kind="ExternalInput").ap()
            for name, a in arrays.items()]
    out_t = nc.dram_tensor("out_t", (C, T * B), F32, kind="ExternalOutput").ap()
    gru_moe_program(nc, *args, out_t)
    result = _run(nc, [arrays], core_ids=[0])
    return np.ascontiguousarray(np.asarray(result.results[0]["out_t"]).reshape(C, T, B).transpose(2, 1, 0))
```
